# Optimizing a Trainium2 kernel written in Bass

```python
import numpy as np
import jax
import jax.numpy as jnp

def _softmax(x, axis=-1):
    return jax.nn.softmax(x, axis=axis)
def _gelu(x):
    return jax.nn.gelu(x, approximate=True)
def _silu(x):
    return jax.nn.silu(x)
def _sigmoid(x):
    return jax.nn.sigmoid(x)
def _layernorm(x, axis=-1, eps=1e-5):
    m = jnp.mean(x, axis=axis, keepdims=True)
    v = jnp.var(x, axis=axis, keepdims=True)
    return (x - m) / jnp.sqrt(v + eps)
def _scatter_add(tgt, idx, src, axis=0):
    return tgt.at[idx].add(src)
def _segment_sum(src, seg, n):
    return jax.ops.segment_sum(src, seg, n)

kernel_name = 'mk_adj_resnorm_d1_adj_1024_871dae'

def setup_inputs(seed: int = 0):
    np.random.seed(seed)
    _w = jnp.asarray
    def _rec_inputs():
        import jax
        import jax.numpy as jnp
        _gk = jax.random.key(seed)
        x = -0.0002928 + 1 * jax.random.normal(jax.random.fold_in(_gk, 1), (4096, 1024), jnp.float32)
        _a = jax.random.bernoulli(jax.random.fold_in(_gk, 2), 0.00195312, (4096, 4096))
        _af = _a.astype(jnp.float32)
        adj = _af
        return x, adj
    x, adj = _rec_inputs()
    def _L0_gnn_setup():
        import jax, jax.numpy as jnp
        import numpy as np
        N = 4096
        D_IN = 1024
        H = 16
        DH = D_IN // H
        ALPHA = 0.2
        MASK_VAL = -65500.0
        key = jax.random.key(seed)
        ks = jax.random.split(key, 7)
        x = jax.random.normal(ks[0], (N, D_IN), dtype=jnp.float32)
        adj = jax.random.randint(ks[1], (N, N), 0, 2).astype(jnp.float32)
        s = 1.0 / np.sqrt(D_IN)
        W_seq = jax.random.normal(ks[2], (D_IN, D_IN), dtype=jnp.float32) * s
        a1 = jax.random.normal(ks[3], (DH,), dtype=jnp.float32) / np.sqrt(DH)
        a2 = jax.random.normal(ks[4], (DH,), dtype=jnp.float32) / np.sqrt(DH)
        W_out = jax.random.normal(ks[5], (D_IN, D_IN), dtype=jnp.float32) * s
        b_out = jax.random.normal(ks[6], (D_IN,), dtype=jnp.float32) * 0.01
        return {'x': x, 'adj': adj, 'W_seq': W_seq, 'a1': a1, 'a2': a2, 'W_out': W_out, 'b_out': b_out}
    _L0_gnn_all = _L0_gnn_setup()
    _L0_gnn_in = {k: v for k, v in _L0_gnn_all.items() if k in ('W_seq', 'a1', 'a2', 'W_out', 'b_out', )}
    del _L0_gnn_all

    return {
        "x": x,
        "adj": adj,
        "L0_gnn_W_seq": _L0_gnn_in["W_seq"],
        "L0_gnn_a1": _L0_gnn_in["a1"],
        "L0_gnn_a2": _L0_gnn_in["a2"],
        "L0_gnn_W_out": _L0_gnn_in["W_out"],
        "L0_gnn_b_out": _L0_gnn_in["b_out"],
    }

def reference(x, adj, L0_gnn_W_seq, L0_gnn_a1, L0_gnn_a2, L0_gnn_W_out, L0_gnn_b_out):
    import jax
    import jax.numpy as jnp
    def _L0_gnn_ref(x, adj, W_seq, a1, a2, W_out, b_out):
        import jax, jax.numpy as jnp
        import numpy as np
        N = 4096
        D_IN = 1024
        H = 16
        DH = D_IN // H
        ALPHA = 0.2
        MASK_VAL = -65500.0
        seq = (x @ W_seq).reshape(N, H, DH)
        score1 = jnp.einsum('nhd,d->hn', seq, a1)
        score2 = jnp.einsum('nhd,d->hn', seq, a2)
        scores = score1[:, :, None] + score2[:, None, :]
        scores = jax.nn.leaky_relu(scores, negative_slope=ALPHA)
        scores = scores + (1.0 - adj)[None, :, :] * MASK_VAL
        attn = jax.nn.softmax(scores, axis=-1)
        hidden = jnp.einsum('hij,jhd->ihd', attn, seq).reshape(N, D_IN)
        hidden = hidden @ W_out + b_out
        return jax.nn.elu(hidden)

    x = _layernorm(x + _L0_gnn_ref(x, adj, L0_gnn_W_seq, L0_gnn_a1, L0_gnn_a2, L0_gnn_W_out, L0_gnn_b_out), axis=-1)
    return x


_drawn_inputs = setup_inputs


def setup_inputs(seed=0):
    import zlib

    import numpy as np

    out = dict(_drawn_inputs(seed))
    spreads = {}
    factors = {'L0_gnn_b_out': 6.668}
    for name, (base, spread) in spreads.items():
        noise = np.random.default_rng([zlib.crc32(name.encode()), seed]).standard_normal(out[name].shape)
        drawn = base * np.exp(spread * noise) if base else spread * noise
        out[name] = jnp.asarray(drawn.astype(out[name].dtype))
    for name, factor in factors.items():
        out[name] = (out[name] * factor).astype(out[name].dtype)
    return out
```

```python
from contextlib import ExitStack

import concourse.bass as bass
from concourse import mybir

ALU = mybir.AluOpType
ACT = mybir.ActivationFunctionType
AX = mybir.AxisListType
F32 = mybir.dt.float32
F16 = mybir.dt.float16
BF16 = mybir.dt.bfloat16

P = 128
HEADS = 16
ALPHA = 0.2
EPS = 1e-5
LIFT = 256.0
STEP_GAIN = 2.0 ** 60


def gat_layer(nc, x, adj, w_seq, a1, a2, w_out, b_out, out):
    N, D = x.shape
    DH = D // HEADS
    NT = N // P
    KT = D // P
    SEQ = D + 2 * HEADS
    SC = SEQ // 3
    AUG = DH + 1
    HALF = 2 * AUG
    XC = 2 * HALF
    IT = 4
    IB = IT * P
    NB = N // IB
    GJ = 8
    NG = NT // GJ
    JA = 5
    ACCW = XC + HALF

    seq_d = nc.dram_tensor("seq_scratch", (N, SEQ), F32).ap()
    adjT_d = nc.dram_tensor("adjT_scratch", (NT, P, NT * P), BF16).ap()
    table_d = nc.dram_tensor("table_scratch", (HEADS, P, NT * XC), F16).ap()
    s1row_d = nc.dram_tensor("score1_rows_scratch", (HEADS * NT, P), F32).ap()
    hid_d = nc.dram_tensor("hidden_scratch", (N, D), F32).ap()

    outer = ExitStack()
    with outer:
        def keep(name, shape, dt):
            return outer.enter_context(nc.sbuf_tensor(name, shape, dt))

        identf = keep("identf", [P, P], F32)
        identb = keep("identb", [P, P], BF16)
        ones16 = keep("ones16", [HEADS, P], F32)
        row_ac = keep("row_ac", [P, 2, NT, HEADS], F32)
        neg_s2 = keep("neg_s2", [P, NT, HEADS], F32)
        step_bias = keep("step_bias", [P, NT, HEADS], F32)

        project_and_transpose(nc, x, adj, w_seq, a1, a2, seq_d, adjT_d, identf, identb, ones16,
                              N, D, DH, NT, KT, SEQ, SC)
        tables(nc, seq_d, table_d, s1row_d, identf, ones16, row_ac, neg_s2, step_bias,
               N, D, DH, NT, SEQ, AUG, HALF, XC)
        attention(nc, adjT_d, table_d, s1row_d, hid_d, row_ac, neg_s2, step_bias,
                  N, D, DH, NT, AUG, HALF, XC, IT, IB, NB, GJ, NG, JA, ACCW)
        output_layer(nc, x, w_out, b_out, hid_d, out, identf, N, D, NT, KT)


def project_and_transpose(nc, x, adj, w_seq, a1, a2, seq_d, adjT_d, identf, identb, ones16,
                          N, D, DH, NT, KT, SEQ, SC):
    BLK = 8
    NQ = NT // BLK
    with ExitStack() as ctx:
        def sb(name, shape, dt):
            return ctx.enter_context(nc.sbuf_tensor(name, shape, dt))

        def ps(name, shape, dt):
            return ctx.enter_context(nc.psum_tensor(name, shape, dt))

        def sem(name):
            return ctx.enter_context(nc.semaphore(name))

        w = sb("w", [P, KT, SEQ], F32)
        avec = sb("avec", [P, 2, DH], F32)
        wa_tmp = sb("wa_tmp", [P, HEADS, DH], F32)
        xin = sb("xin", [P, 2, D], F32)
        xT = sb("xT", [P, 2, KT, P], F32)
        adj_in = sb("adj_in", [P, 2, N], F32)
        adj_b = sb("adj_b", [P, 2, N], BF16)
        degree = sb("degree", [P, 2], F32)
        no_edge = sb("no_edge", [P, 2], F32)
        adjT = sb("adjT", [P, 2, NT, P], BF16)
        seq = sb("seq", [P, 2, SEQ], F32)
        xT_ps = ps("xT_ps", [P, KT, P], F32)
        adjT_ps = ps("adjT_ps", [P, 2, BLK, P], BF16)
        seq_ps = ps("seq_ps", [P, 3, 512], F32)

        ident_made = sem("ident_made")
        w_in = sem("w_in")
        a_in = sem("a_in")
        wa_mul = sem("wa_mul")
        wa_sum = sem("wa_sum")
        x_in = [sem("x_in0"), sem("x_in1")]
        adj_arrived = [sem("adj_in0"), sem("adj_in1")]
        x_turned = sem("x_turned")
        xT_copied = sem("xT_copied")
        adj_cast = sem("adj_cast")
        no_edge_found = sem("no_edge_found")
        adj_fixed = sem("adj_fixed")
        adj_turned = sem("adj_turned")
        adjT_copied = sem("adjT_copied")
        seq_done = sem("seq_done")
        seq_copied = sem("seq_copied")
        seq_out = [sem("seq_out0"), sem("seq_out1")]
        adjT_out = [sem("adjT_out0"), sem("adjT_out1")]

        block = ctx.enter_context(nc.Block())

        @block.gpsimd
        def _(pool):
            pool.memset(identf[:, :], 0.0).then_inc(ident_made, 1)
            pool.memset(identb[:, :], 0.0).then_inc(ident_made, 1)
            pool.memset(ones16[:, :], 1.0).then_inc(ident_made, 1)
            pool.wait_ge(ident_made, 3)
            for m in (identf, identb):
                pool.affine_select(out=m[:, :], in_=m[:, :], compare_op=ALU.not_equal, fill=1.0,
                                   base=0, pattern=[[-1, P]], channel_multiplier=1).then_inc(ident_made, 1)

        @block.sync
        def _(sp):
            sp.dma_start(avec[:, 0, :], a2.partition_broadcast(P)).then_inc(a_in, 16)
            sp.dma_start(avec[:, 1, :], a1.partition_broadcast(P)).then_inc(a_in, 16)
            for k in range(KT):
                sp.dma_start(w[:, k, 0:D], w_seq[k * P:(k + 1) * P, :]).then_inc(w_in, 16)

            def loads(t, tt, par, first):
                if not first:
                    sp.wait_ge(x_turned, t - 1)
                sp.dma_start(xin[:, par, :], x[bass.ds(t * P, P), :]).then_inc(x_in[par], 16)
                if not first:
                    sp.wait_ge(adj_cast, t - 1)
                sp.dma_start(adj_in[:, par, :], adj[bass.ds(t * P, P), :]).then_inc(adj_arrived[par], 16)

            def stores(t, par):
                sp.wait_ge(seq_copied, t + 1)
                sp.dma_start(seq_d[bass.ds(t * P, P), :], seq[:, par, :]).then_inc(seq_out[par], 16)
                sp.wait_ge(adjT_copied, NQ * (t + 1))
                sp.dma_start(adjT_d[bass.ds(t, 1), :, :].rearrange("o p f -> (o p) f"),
                             adjT[:, par, :, :].rearrange("p j i -> p (j i)")).then_inc(adjT_out[par], 16)

            loads(0, 0, 0, True)
            loads(1, 0, 1, True)
            stores(0, 0)
            with sp.Fori(1, NT // 2) as tt:
                loads(2 * tt, tt, 0, False)
                stores(2 * tt - 1, 1)
                loads(2 * tt + 1, tt, 1, False)
                stores(2 * tt, 0)
            stores(NT - 1, 1)
            for par in range(2):
                sp.wait_ge(seq_out[par], 16 * (NT // 2))
                sp.wait_ge(adjT_out[par], 16 * (NT // 2))

        @block.tensor
        def _(pe):
            pe.wait_ge(ident_made, 5)

            def tile(t, tt, par, first, very_first):
                pe.wait_ge(x_in[par], 16 * (tt + 1))
                if not very_first:
                    pe.wait_ge(xT_copied, t)
                for k in range(KT):
                    mm = pe.transpose(xT_ps[:, k, :], xin[:, par, k * P:(k + 1) * P], identf[:, :])
                mm.then_inc(x_turned, 1)
                pe.wait_ge(adj_fixed, t + 1)
                for q in range(NQ):
                    if not (very_first and q < 2):
                        pe.wait_ge(adjT_copied, NQ * t + q - 1)
                    for b in range(BLK):
                        j = q * BLK + b
                        mm = pe.transpose(adjT_ps[:, q % 2, b, :], adj_b[:, par, j * P:(j + 1) * P], identb[:, :])
                    mm.then_inc(adj_turned, 1)
                if very_first:
                    pe.wait_ge(w_in, 16 * KT)
                    pe.wait_ge(wa_sum, 2 * KT)
                else:
                    pe.wait_ge(seq_copied, t)
                pe.wait_ge(xT_copied, t + 1)
                for k in range(KT):
                    for c in range(3):
                        mm = pe.matmul(seq_ps[:, c, 0:SC], xT[:, par, k, :], w[:, k, c * SC:(c + 1) * SC],
                                       start=(k == 0), stop=(k == KT - 1))
                mm.then_inc(seq_done, 1)

            tile(0, 0, 0, True, True)
            tile(1, 0, 1, True, False)
            with pe.Fori(1, NT // 2) as tt:
                tile(2 * tt, tt, 0, False, False)
                tile(2 * tt + 1, tt, 1, False, False)

        @block.vector
        def _(dve):
            dve.wait_ge(a_in, 32)
            n = 0
            dve.wait_ge(w_in, 16 * KT)
            for k in range(KT):
                for s in range(2):
                    if n:
                        dve.wait_ge(wa_sum, n)
                    dve.tensor_tensor(wa_tmp[:, :, :], w[:, k, 0:D].rearrange("p (h d) -> p h d", h=HEADS),
                                      avec[:, s:s + 1, :].broadcast_to([P, HEADS, DH]), ALU.mult).then_inc(wa_mul, 1)
                    n += 1
                    dve.wait_ge(wa_mul, n)
                    dve.tensor_reduce(w[:, k, D + s * HEADS:D + (s + 1) * HEADS], wa_tmp[:, :, :],
                                      AX.X, ALU.add).then_inc(wa_sum, 1)

            def tile(t, tt, par, first):
                dve.wait_ge(x_turned, t + 1)
                if not first:
                    dve.wait_ge(seq_done, t - 1)
                dve.tensor_copy(xT[:, par, :, :], xT_ps[:, :, :]).then_inc(xT_copied, 1)
                dve.wait_ge(adj_cast, t + 1)
                dve.tensor_scalar(no_edge[:, par:par + 1], degree[:, par:par + 1], 0.0, None,
                                  ALU.is_equal).then_inc(no_edge_found, 1)
                dve.wait_ge(no_edge_found, t + 1)
                dve.tensor_scalar(adj_b[:, par, :], adj_b[:, par, :], no_edge[:, par:par + 1], None,
                                  ALU.max).then_inc(adj_fixed, 1)
                if not first:
                    dve.wait_ge(adjT_out[par], 16 * tt)
                for q in range(NQ):
                    dve.wait_ge(adj_turned, NQ * t + q + 1)
                    dve.tensor_copy(adjT[:, par, q * BLK:(q + 1) * BLK, :],
                                    adjT_ps[:, q % 2, :, :]).then_inc(adjT_copied, 1)

            tile(0, 0, 0, True)
            tile(1, 0, 1, True)
            with dve.Fori(1, NT // 2) as tt:
                tile(2 * tt, tt, 0, False)
                tile(2 * tt + 1, tt, 1, False)

        @block.scalar
        def _(act):
            def cast(t, tt, par, first):
                act.wait_ge(adj_arrived[par], 16 * (tt + 1))
                if not first:
                    act.wait_ge(adj_turned, NQ * (t - 1))
                act.activation(adj_b[:, par, :], adj_in[:, par, :], ACT.Copy,
                               accum_out=degree[:, par:par + 1]).then_inc(adj_cast, 1)

            def evacuate(t, tt, par, first):
                act.wait_ge(seq_done, t + 1)
                if not first:
                    act.wait_ge(seq_out[par], 16 * tt)
                act.copy(seq[:, par, :].rearrange("p (c s) -> p c s", c=3), seq_ps[:, :, 0:SC]).then_inc(seq_copied, 1)

            cast(0, 0, 0, True)
            cast(1, 0, 1, True)
            evacuate(0, 0, 0, True)
            cast(2, 1, 0, False)
            evacuate(1, 0, 1, True)
            cast(3, 1, 1, False)
            evacuate(2, 1, 0, False)
            with act.Fori(2, NT // 2) as tt:
                cast(2 * tt, tt, 0, False)
                evacuate(2 * tt - 1, tt - 1, 1, False)
                cast(2 * tt + 1, tt, 1, False)
                evacuate(2 * tt, tt, 0, False)
            evacuate(NT - 1, NT // 2 - 1, 1, False)


def tables(nc, seq_d, table_d, s1row_d, identf, ones16, row_ac, neg_s2, step_bias,
           N, D, DH, NT, SEQ, AUG, HALF, XC):
    HQ = P // NT
    with ExitStack() as ctx:
        def sb(name, shape, dt):
            return ctx.enter_context(nc.sbuf_tensor(name, shape, dt))

        def ps(name, shape, dt):
            return ctx.enter_context(nc.psum_tensor(name, shape, dt))

        def sem(name):
            return ctx.enter_context(nc.semaphore(name))

        scores = sb("scores", [P, NT, 2, HEADS], F32)
        part_max = sb("part_max", [P, HEADS], F32)
        head_max = sb("head_max", [HEADS, 1], F32)
        diag_max = sb("diag_max", [HEADS, HEADS], F32)
        max_s2 = sb("max_s2", [P, HEADS], F32)
        shifted = sb("shifted", [P, NT, HEADS], F32)
        bound = sb("bound", [P, NT, HEADS], F32)
        powers = sb("powers", [P, 2, NT, HEADS], F32)
        exps = sb("exps", [P, 2, NT, HEADS], F32)
        expo = sb("expo", [P, 2, NT, HEADS], F32)
        s1_flip = sb("s1_flip", [P, HEADS // HQ, P], F32)
        values = sb("values", [P, 2, NT, DH], F32)
        full = sb("full", [P, 2, NT, HALF], F32)
        table = sb("table", [P, 2, NT, XC], F16)
        small_ps = ps("small_ps", [P, P], F32)
        max_ps = ps("max_ps", [P, HEADS], F32)
        s1_ps = ps("s1_ps", [P, HEADS // HQ, P], F32)

        scores_in = sem("scores_in")
        step = sem("step")
        max_turned = sem("max_turned")
        max_spread = sem("max_spread")
        s1_turned = sem("s1_turned")
        s1_copied = sem("s1_copied")
        expo_ready = sem("expo_ready")
        exp_done = sem("exp_done")
        values_in = [sem("values_in0"), sem("values_in1")]
        full_ready = sem("full_ready")
        parts = sem("parts")
        high_ready = sem("high_ready")
        low_ready = sem("low_ready")
        table_out = [sem("table_out0"), sem("table_out1")]
        s1_out = sem("s1_out")

        block = ctx.enter_context(nc.Block())
        seq_v = seq_d.rearrange("(t p) c -> p t c", p=P)

        @block.sync
        def _(sp):
            sp.dma_start(scores[:, :, :, :].rearrange("p t s h -> p t (s h)"), seq_v[:, :, D:SEQ]).then_inc(scores_in, 16)
            for h in range(HEADS):
                par = h % 2
                if h >= 2:
                    sp.wait_ge(parts, 4 * (h - 1))
                sp.dma_start(values[:, par, :, :], seq_v[:, :, h * DH:(h + 1) * DH]).then_inc(values_in[par], 16)
                if h >= 1:
                    sp.wait_ge(low_ready, h)
                    sp.dma_start(table_d[h - 1, :, :], table[:, 1 - par, :, :].rearrange("p t c -> p (t c)")
                                 ).then_inc(table_out[1 - par], 16)
                if h == 0:
                    sp.wait_ge(s1_copied, 1)
                    sp.dma_start(s1row_d.rearrange("(k q) i -> q k i", q=P), s1_flip[:, :, :]).then_inc(s1_out, 16)
            sp.wait_ge(low_ready, HEADS)
            sp.dma_start(table_d[HEADS - 1, :, :], table[:, 1, :, :].rearrange("p t c -> p (t c)")).then_inc(table_out[1], 16)
            sp.wait_ge(table_out[0], 16 * (HEADS // 2))
            sp.wait_ge(table_out[1], 16 * (HEADS // 2))
            sp.wait_ge(s1_out, 16)

        @block.tensor
        def _(pe):
            pe.wait_ge(step, 2)
            pe.transpose(small_ps[0:HEADS, :], part_max[:, :], identf[:, :]).then_inc(max_turned, 1)
            pe.wait_ge(step, 4)
            pe.matmul(max_ps[:, :], ones16[:, :], diag_max[:, :], start=True, stop=True).then_inc(max_spread, 1)
            for k in range(HEADS // HQ):
                mm = pe.transpose(s1_ps[:, k, :], bound[:, :, :].rearrange("p t h -> p (t h)")[:, k * P:(k + 1) * P],
                                  identf[:, :])
            mm.then_inc(s1_turned, 1)

        @block.vector
        def _(dve):
            s2 = scores[:, :, 0, :]
            s1 = scores[:, :, 1, :]
            dve.wait_ge(scores_in, 16)
            dve.tensor_copy(bound[:, :, :].rearrange("p t h -> p (t h)").rearrange("p (h t) -> p t h", h=HEADS),
                            s1).then_inc(step, 1)
            dve.tensor_reduce(part_max[:, :], s2.rearrange("p t h -> p h t"), AX.X, ALU.max).then_inc(step, 1)
            dve.wait_ge(max_turned, 1)
            dve.tensor_reduce(head_max[:, :], small_ps[0:HEADS, :], AX.X, ALU.max).then_inc(step, 1)
            dve.wait_ge(step, 3)
            dve.tensor_scalar(diag_max[:, :], identf[0:HEADS, 0:HEADS], head_max[:, 0:1], None, ALU.mult).then_inc(step, 1)
            dve.tensor_scalar(neg_s2[:, :, :], s2, -1.0, None, ALU.mult).then_inc(step, 1)
            dve.tensor_scalar(step_bias[:, :, :], s2, -STEP_GAIN, None, ALU.mult).then_inc(step, 1)
            dve.wait_ge(max_spread, 1)
            dve.tensor_copy(max_s2[:, :], max_ps[:, :]).then_inc(step, 1)
            dve.wait_ge(s1_turned, 1)
            dve.tensor_copy(s1_flip[:, :, :], s1_ps[:, :, :]).then_inc(s1_copied, 1)
            dve.wait_ge(step, 7)
            m = max_s2[:, None, :].broadcast_to([P, NT, HEADS])
            dve.tensor_tensor(shifted[:, :, :], s2, m, ALU.subtract).then_inc(step, 1)
            dve.tensor_tensor(bound[:, :, :], s1, m, ALU.add).then_inc(step, 1)
            dve.wait_ge(step, 9)
            dve.tensor_scalar(expo[:, 0, :, :], bound[:, :, :], 0.0, 1.0 - ALPHA, ALU.min, ALU.mult).then_inc(expo_ready, 1)
            dve.tensor_scalar(expo[:, 1, :, :], bound[:, :, :], 0.0, ALPHA - 1.0, ALU.max, ALU.mult).then_inc(expo_ready, 1)
            dve.wait_ge(exp_done, 2)
            dve.tensor_scalar(powers[:, :, :, :], exps[:, :, :, :], LIFT, None, ALU.mult).then_inc(step, 1)
            dve.wait_ge(step, 10)
            for h in range(HEADS):
                par = h % 2
                dve.wait_ge(values_in[par], 16 * (h // 2 + 1))
                if h >= 2:
                    dve.wait_ge(high_ready, h - 1)
                    dve.wait_ge(low_ready, h - 1)
                for s in range(2):
                    f = powers[:, s, :, h:h + 1]
                    dve.tensor_tensor(full[:, par, :, s * AUG:s * AUG + DH], values[:, par, :, :],
                                      f.broadcast_to([P, NT, DH]), ALU.mult).then_inc(parts, 1)
                    dve.tensor_copy(full[:, par, :, s * AUG + DH:(s + 1) * AUG], f).then_inc(parts, 1)
                dve.wait_ge(high_ready, h + 1)
                dve.tensor_tensor(table[:, par, :, HALF:XC], full[:, par, :, :], table[:, par, :, 0:HALF],
                                  ALU.subtract).then_inc(low_ready, 1)

        @block.scalar
        def _(act):
            act.wait_ge(step, 9)
            act.activation(exps[:, 0, :, :], shifted[:, :, :], ACT.Exp).then_inc(exp_done, 1)
            act.activation(exps[:, 1, :, :], shifted[:, :, :], ACT.Exp, scale=ALPHA).then_inc(exp_done, 1)
            act.wait_ge(expo_ready, 2)
            act.activation(row_ac[:, :, :, :], expo[:, :, :, :], ACT.Exp)
            for h in range(HEADS):
                par = h % 2
                act.wait_ge(parts, 4 * (h + 1))
                if h >= 2:
                    act.wait_ge(table_out[par], 16 * (h // 2))
                act.copy(table[:, par, :, 0:HALF], full[:, par, :, :]).then_inc(high_ready, 1)


def attention(nc, adjT_d, table_d, s1row_d, hid_d, row_ac, neg_s2, step_bias,
              N, D, DH, NT, AUG, HALF, XC, IT, IB, NB, GJ, NG, JA, ACCW):
    with ExitStack() as ctx:
        def sb(name, shape, dt):
            return ctx.enter_context(nc.sbuf_tensor(name, shape, dt))

        def sem(name):
            return ctx.enter_context(nc.semaphore(name))

        adjT = sb("adjT_blk", [P, 2, IT, NT, P], BF16)
        table = sb("table_h", [P, 2, NT, XC], F16)
        s1 = sb("score1_row", [P, 2, IB], F32)
        below = sb("below", [P, 2, JA, IB], BF16)
        mask = sb("mask", [P, 2, GJ, IB], BF16)
        sums = sb("sums", [P, IT, ACCW], F32)
        mixed = sb("mixed", [P, IT, HALF], F32)
        posit = sb("posit", [P, IT, AUG], F32)
        recip = sb("recip", [P, IT], F32)
        hidden = sb("hidden", [P, 2, IT, D], F32)
        acc = ctx.enter_context(nc.psum_tensor("acc", [P, 2, IT, 512], F32))

        adjT_in = [sem("adjT_in0"), sem("adjT_in1")]
        table_in = [sem("table_in0"), sem("table_in1")]
        s1_in = [sem("s1_in0"), sem("s1_in1")]
        below_ready = sem("below_ready")
        stt_ready = sem("stt_ready")
        mask_ready = sem("mask_ready")
        mask_used = sem("mask_used")
        sums_copied = sem("sums_copied")
        post = sem("post")
        hid_out = [sem("hid_out0"), sem("hid_out1")]

        block = ctx.enter_context(nc.Block())
        adjT_v = adjT_d.rearrange("(b i) p f -> b p i f", i=IT)
        s1_v = s1row_d.rearrange("(h b i) c -> b h (i c)", h=HEADS, i=IT)
        hid_v = hid_d.rearrange("(b i p) d -> b p i d", i=IT, p=P)
        POST = 8

        @block.sync
        def _(sp):
            def load_head(q, b, h, hp, first):
                if not first:
                    sp.wait_ge(mask_used, NG * (q - 1))
                sp.dma_start(table[:, hp, :, :].rearrange("p t c -> p (t c)"),
                             table_d[bass.ds(h, 1), :, :].rearrange("o p f -> (o p) f")).then_inc(table_in[hp], 16)
                sp.dma_start(s1[:, hp, :], s1_v[bass.ds(b, 1), bass.ds(h, 1), :].rearrange("a b c -> (a b c)")
                             .partition_broadcast(P)).then_inc(s1_in[hp], 16)

            def load_adj(b, bp, first):
                if not first:
                    sp.wait_ge(mask_used, NG * HEADS * (b - 1))
                sp.dma_start(adjT[:, bp, :, :, :].rearrange("p i j c -> p i (j c)"),
                             adjT_v[bass.ds(b, 1), :, :, :].rearrange("o p i f -> (o p) i f")).then_inc(adjT_in[bp], 16)

            def store(b, bp):
                sp.wait_ge(post, POST * HEADS * (b + 1))
                sp.dma_start(hid_v[bass.ds(b, 1), :, :, :].rearrange("o p i d -> (o p) i d"),
                             hidden[:, bp, :, :]).then_inc(hid_out[bp], 16)

            def heads(b, first):
                for hp in range(2):
                    load_head(b * HEADS + hp, b, hp, hp, first)
                with sp.Fori(1, HEADS // 2) as hh:
                    for hp in range(2):
                        load_head(b * HEADS + 2 * hh + hp, b, 2 * hh + hp, hp, False)

            load_adj(0, 0, True)
            heads(0, True)
            load_adj(1, 1, True)
            heads(1, False)
            store(0, 0)
            with sp.Fori(1, NB // 2) as bb:
                load_adj(2 * bb, 0, False)
                heads(2 * bb, False)
                store(2 * bb - 1, 1)
                load_adj(2 * bb + 1, 1, False)
                heads(2 * bb + 1, False)
                store(2 * bb, 0)
            store(NB - 1, 1)
            sp.wait_ge(hid_out[0], 16 * (NB // 2))
            sp.wait_ge(hid_out[1], 16 * (NB // 2))

        @block.tensor
        def _(pe):
            def head(q, hp, bp, uses, first):
                pe.wait_ge(table_in[hp], 16 * (uses + 1))
                for g in range(NG):
                    pe.wait_ge(mask_ready, NG * q + g + 1)
                    if g == 0 and not first:
                        pe.wait_ge(sums_copied, q - 1)
                    for jj in range(GJ):
                        j = g * GJ + jj
                        for i in range(IT):
                            pe.matmul(acc[:, hp, i, 0:XC], mask[:, g % 2, jj, i * P:(i + 1) * P], table[:, hp, j, :],
                                      start=(j == 0), stop=(j == NT - 1), skip_group_check=True)
                            mm = pe.matmul(acc[:, hp, i, XC:ACCW].rearrange("p (s c) -> p s c", s=2),
                                           adjT[:, bp, i, j, :],
                                           table[:, hp, j, :].rearrange("p (s c) -> p s c", s=2)[:, :, 0:AUG],
                                           start=False, stop=(j == NT - 1), skip_group_check=True)
                    mm.then_inc(mask_used, 1)

            def blk(b, bb, bp, first):
                pe.wait_ge(adjT_in[bp], 16 * (bb + 1))
                for hp in range(2):
                    head(b * HEADS + hp, hp, bp, b * (HEADS // 2), first)
                with pe.Fori(1, HEADS // 2) as hh:
                    for hp in range(2):
                        head(b * HEADS + 2 * hh + hp, hp, bp, b * (HEADS // 2) + hh, False)

            blk(0, 0, 0, True)
            blk(1, 0, 1, False)
            with pe.Fori(1, NB // 2) as bb:
                blk(2 * bb, bb, 0, False)
                blk(2 * bb + 1, bb, 1, False)

        @block.vector
        def _(dve):
            def masks(q, h, hp, bp, uses, g, first):
                n = NG * q + g
                if not (first and g < 2):
                    dve.wait_ge(mask_used, n - 1)
                for jj in range(JA, GJ):
                    j = g * GJ + jj
                    ins = dve.scalar_tensor_tensor(
                        mask[:, g % 2, jj, :].rearrange("p (i c) -> p i c", i=IT),
                        s1[:, hp, :].rearrange("p (i c) -> p i c", i=IT), neg_s2[:, j, bass.ds(h, 1)],
                        adjT[:, bp, :, j, :], ALU.is_lt, ALU.mult)
                ins.then_inc(stt_ready, 1)
                dve.wait_ge(below_ready, n + 1)
                dve.tensor_tensor(
                    mask[:, g % 2, 0:JA, :].rearrange("p j (i c) -> p j i c", i=IT),
                    below[:, g % 2, :, :].rearrange("p j (i c) -> p j i c", i=IT),
                    adjT[:, bp, :, g * GJ:g * GJ + JA, :].rearrange("p i j c -> p j i c"), ALU.mult).then_inc(mask_ready, 1)

            def combine(q, b, h, bp):
                n = POST * q
                row_a = row_ac[:, 0, bass.ds(b * IT, IT), bass.ds(h, 1)]
                row_c = row_ac[:, 1, bass.ds(b * IT, IT), bass.ds(h, 1)]
                dve.wait_ge(sums_copied, q + 1)
                dve.tensor_tensor(mixed[:, :, :], sums[:, :, 0:HALF], sums[:, :, HALF:XC], ALU.add).then_inc(post, 1)
                dve.tensor_tensor(posit[:, :, :], sums[:, :, XC:XC + AUG], sums[:, :, XC + AUG:ACCW], ALU.add).then_inc(post, 1)
                dve.wait_ge(post, n + 2)
                dve.tensor_tensor(posit[:, :, :], posit[:, :, :], mixed[:, :, 0:AUG], ALU.subtract).then_inc(post, 1)
                dve.tensor_tensor(mixed[:, :, AUG:HALF], mixed[:, :, AUG:HALF],
                                  row_c.broadcast_to([P, IT, AUG]), ALU.mult).then_inc(post, 1)
                dve.wait_ge(post, n + 4)
                dve.tensor_tensor(posit[:, :, :], posit[:, :, :], row_a.broadcast_to([P, IT, AUG]), ALU.mult).then_inc(post, 1)
                dve.wait_ge(post, n + 5)
                dve.tensor_tensor(posit[:, :, :], posit[:, :, :], mixed[:, :, AUG:HALF], ALU.add).then_inc(post, 1)
                dve.wait_ge(post, n + 6)
                dve.reciprocal(recip[:, :], posit[:, :, DH]).then_inc(post, 1)
                dve.wait_ge(post, n + 7)
                dve.tensor_tensor(hidden[:, bp, :, bass.ds(h * DH, DH)], posit[:, :, 0:DH],
                                  recip[:, :, None].broadcast_to([P, IT, DH]), ALU.mult).then_inc(post, 1)

            def head(q, b, h, hp, bp, uses, first, alone):
                dve.wait_ge(s1_in[hp], 16 * (uses + 1))
                for g in range(NG):
                    masks(q, h, hp, bp, uses, g, first)
                    if g == 1 and not alone:
                        combine(q - 1, b, h - 1, bp)

            def blk(b, bb, bp, first, reused):
                dve.wait_ge(adjT_in[bp], 16 * (bb + 1))
                for hp in range(2):
                    if hp == 1 and reused:
                        dve.wait_ge(hid_out[bp], 16 * bb)
                    head(b * HEADS + hp, b, hp, hp, bp, b * (HEADS // 2), first and hp == 0, hp == 0)
                with dve.Fori(1, HEADS // 2) as hh:
                    for hp in range(2):
                        head(b * HEADS + 2 * hh + hp, b, 2 * hh + hp, hp, bp, b * (HEADS // 2) + hh, False, False)
                combine(b * HEADS + HEADS - 1, b, HEADS - 1, bp)

            blk(0, 0, 0, True, False)
            blk(1, 0, 1, False, False)
            with dve.Fori(1, NB // 2) as bb:
                blk(2 * bb, bb, 0, False, True)
                blk(2 * bb + 1, bb, 1, False, True)

        @block.scalar
        def _(act):
            def evacuate(q, hp, first):
                act.wait_ge(mask_used, NG * (q + 1))
                if not first:
                    act.wait_ge(post, POST * (q - 1) + 2)
                act.copy(sums[:, :, :], acc[:, hp, :, 0:ACCW]).then_inc(sums_copied, 1)

            def head(q, h, hp, uses, first, alone, second):
                act.wait_ge(s1_in[hp], 16 * (uses + 1))
                for g in range(NG):
                    if not (first and g < 2):
                        act.wait_ge(mask_ready, NG * q + g - 1)
                    for jj in range(JA):
                        ins = act.activation(below[:, g % 2, jj, :], s1[:, hp, :], ACT.Sigmoid,
                                             bias=step_bias[:, g * GJ + jj, bass.ds(h, 1)], scale=-STEP_GAIN)
                    ins.then_inc(below_ready, 1)
                    if g == 0 and not alone:
                        evacuate(q - 1, 1 - hp, second)

            def blk(b, first):
                for hp in range(2):
                    head(b * HEADS + hp, hp, hp, b * (HEADS // 2), first and hp == 0, hp == 0, first and hp == 1)
                with act.Fori(1, HEADS // 2) as hh:
                    for hp in range(2):
                        head(b * HEADS + 2 * hh + hp, 2 * hh + hp, hp, b * (HEADS // 2) + hh, False, False, False)
                evacuate(b * HEADS + HEADS - 1, 1, False)

            blk(0, True)
            blk(1, False)
            with act.Fori(1, NB // 2) as bb:
                blk(2 * bb, False)
                blk(2 * bb + 1, False)


def output_layer(nc, x, w_out, b_out, hid_d, out, identf, N, D, NT, KT):
    CH = D // 512
    with ExitStack() as ctx:
        def sb(name, shape, dt):
            return ctx.enter_context(nc.sbuf_tensor(name, shape, dt))

        def sem(name):
            return ctx.enter_context(nc.semaphore(name))

        w = sb("w_out_sb", [P, KT, D], F32)
        bias = sb("bias", [P, D], F32)
        hid = sb("hid", [P, 2, D], F32)
        xin = sb("x_res", [P, 2, D], F32)
        hT = sb("hT", [P, 2, KT, P], F32)
        z = sb("z", [P, 2, D], F32)
        neg = sb("neg", [P, 2, D], F32)
        e = sb("e", [P, 2, D], F32)
        y = sb("y", [P, 2, D], F32)
        fin = sb("fin", [P, 2, D], F32)
        pos = sb("pos", [P, 2, D], F32)
        stats = sb("stats", [P, 2, CH, 6], F32)
        mv = sb("mv", [P, 2, 2], F32)
        var = sb("var", [P, 2], F32)
        rstd = sb("rstd", [P, 2], F32)
        hT_ps = ctx.enter_context(nc.psum_tensor("hT_ps", [P, KT, P], F32))
        z_ps = ctx.enter_context(nc.psum_tensor("z_ps", [P, 2, CH, 512], F32))

        half = sb("half", [P, 2], F32)
        w_in = sem("w_out_in")
        b_in = sem("b_in")
        const_made = sem("const_made")
        hid_in = [sem("hid_in0"), sem("hid_in1")]
        x_in = [sem("x_res0"), sem("x_res1")]
        h_turned = sem("h_turned")
        hT_copied = sem("hT_copied")
        z_done = sem("z_done")
        z_ready = sem("z_ready")
        neg_ready = sem("neg_ready")
        exp_ready = sem("exp_ready")
        pos_ready = sem("pos_ready")
        y_ready = sem("y_ready")
        stats_ready = sem("stats_ready")
        mv_ready = sem("mv_ready")
        var_ready = sem("var_ready")
        rstd_ready = sem("rstd_ready")
        fin_ready = sem("fin_ready")
        out_stored = [sem("out0"), sem("out1")]

        block = ctx.enter_context(nc.Block())

        @block.sync
        def _(sp):
            sp.dma_start(bias[:, :], b_out.partition_broadcast(P)).then_inc(b_in, 16)
            for k in range(KT):
                sp.dma_start(w[:, k, :], w_out[k * P:(k + 1) * P, :]).then_inc(w_in, 16)

            def loads(t, par, first):
                if not first:
                    sp.wait_ge(h_turned, t - 1)
                sp.dma_start(hid[:, par, :], hid_d[bass.ds(t * P, P), :]).then_inc(hid_in[par], 16)
                if not first:
                    sp.wait_ge(pos_ready, t - 1)
                sp.dma_start(xin[:, par, :], x[bass.ds(t * P, P), :]).then_inc(x_in[par], 16)

            def store(t, par):
                sp.wait_ge(fin_ready, t + 1)
                sp.dma_start(out[bass.ds(t * P, P), :], fin[:, par, :]).then_inc(out_stored[par], 16)

            loads(0, 0, True)
            loads(1, 1, True)
            with sp.Fori(1, NT // 2) as tt:
                for par in range(2):
                    loads(2 * tt + par, par, False)
                    store(2 * tt + par - 2, par)
            store(NT - 2, 0)
            store(NT - 1, 1)
            sp.wait_ge(out_stored[0], 16 * (NT // 2))
            sp.wait_ge(out_stored[1], 16 * (NT // 2))

        @block.tensor
        def _(pe):
            def turn(t, tt, par, very_first):
                pe.wait_ge(hid_in[par], 16 * (tt + 1))
                if not very_first:
                    pe.wait_ge(hT_copied, t)
                for k in range(KT):
                    mm = pe.transpose(hT_ps[:, k, :], hid[:, par, k * P:(k + 1) * P], identf[:, :])
                mm.then_inc(h_turned, 1)

            def project(t, par, first):
                pe.wait_ge(hT_copied, t + 1)
                if not first:
                    pe.wait_ge(z_ready, t - 1)
                for k in range(KT):
                    for c in range(CH):
                        mm = pe.matmul(z_ps[:, par, c, :], hT[:, par, k, :], w[:, k, c * 512:(c + 1) * 512],
                                       start=(k == 0), stop=(k == KT - 1))
                mm.then_inc(z_done, 1)

            turn(0, 0, 0, True)
            pe.wait_ge(w_in, 16 * KT)
            turn(1, 0, 1, False)
            project(0, 0, True)
            turn(2, 1, 0, False)
            project(1, 1, True)
            turn(3, 1, 1, False)
            project(2, 0, False)
            with pe.Fori(2, NT // 2) as tt:
                turn(2 * tt, tt, 0, False)
                project(2 * tt - 1, 1, False)
                turn(2 * tt + 1, tt, 1, False)
                project(2 * tt, 0, False)
            project(NT - 1, 1, False)

        @block.vector
        def _(dve):
            def copy_hT(t, par, first):
                dve.wait_ge(h_turned, t + 1)
                if not first:
                    dve.wait_ge(z_done, t - 1)
                dve.tensor_copy(hT[:, par, :, :], hT_ps[:, :, :]).then_inc(hT_copied, 1)

            def finish(t, tt, par, first):
                dve.wait_ge(rstd_ready, t + 1)
                if not first:
                    dve.wait_ge(out_stored[par], 16 * tt)
                dve.tensor_scalar(fin[:, par, :], y[:, par, :], mv[:, par, 0:1], rstd[:, par:par + 1],
                                  ALU.subtract, ALU.mult).then_inc(fin_ready, 1)

            def tile(t, tt, par, first, very_first, last):
                if not last:
                    copy_hT(t + 1, 1 - par, very_first)
                dve.wait_ge(z_done, t + 1)
                dve.tensor_tensor(z[:, par, :].rearrange("p (c f) -> p c f", c=CH), z_ps[:, par, :, :],
                                  bias[:, :].rearrange("p (c f) -> p c f", c=CH), ALU.add).then_inc(z_ready, 1)
                dve.wait_ge(z_ready, t + 1)
                dve.tensor_scalar(neg[:, par, :], z[:, par, :], 0.0, None, ALU.min).then_inc(neg_ready, 1)
                dve.wait_ge(x_in[par], 16 * (tt + 1))
                dve.scalar_tensor_tensor(pos[:, par, :], z[:, par, :], 0.0, xin[:, par, :],
                                         ALU.max, ALU.add).then_inc(pos_ready, 1)
                if not very_first:
                    finish(t - 1, tt if par else tt - 1, 1 - par, first)
                dve.wait_ge(exp_ready, t + 1)
                dve.wait_ge(pos_ready, t + 1)
                dve.scalar_tensor_tensor(y[:, par, :], e[:, par, :], -1.0, pos[:, par, :],
                                         ALU.add, ALU.add).then_inc(y_ready, 1)
                dve.wait_ge(y_ready, t + 1)
                for c in range(CH):
                    dve.bn_stats(stats[:, par, c, :], y[:, par, c * 512:(c + 1) * 512]).then_inc(stats_ready, 1)
                dve.drain()
                dve.bn_aggr(mv[:, par, :], stats[:, par, :, :]).then_inc(mv_ready, 1)
                dve.wait_ge(mv_ready, t + 1)
                dve.tensor_scalar(var[:, par:par + 1], mv[:, par, 1:2], EPS, None, ALU.add).then_inc(var_ready, 1)

            dve.wait_ge(b_in, 16)
            copy_hT(0, 0, True)
            tile(0, 0, 0, True, True, False)
            tile(1, 0, 1, True, False, False)
            tile(2, 1, 0, True, False, False)
            tile(3, 1, 1, False, False, False)
            with dve.Fori(2, NT // 2 - 1) as tt:
                tile(2 * tt, tt, 0, False, False, False)
                tile(2 * tt + 1, tt, 1, False, False, False)
            tile(NT - 2, NT // 2 - 1, 0, False, False, False)
            tile(NT - 1, NT // 2 - 1, 1, False, False, True)
            finish(NT - 1, NT // 2 - 1, 1, False)

        @block.scalar
        def _(act):
            def tile(t, par, first):
                act.wait_ge(neg_ready, t + 1)
                if not first:
                    act.wait_ge(y_ready, t - 1)
                act.activation(e[:, par, :], neg[:, par, :], ACT.Exp).then_inc(exp_ready, 1)

            tile(0, 0, True)
            tile(1, 1, True)
            with act.Fori(1, NT // 2) as tt:
                tile(2 * tt, 0, False)
                tile(2 * tt + 1, 1, False)

        @block.gpsimd
        def _(pool):
            pool.memset(half[:, 0:1], -0.5).then_inc(const_made, 1)
            pool.wait_ge(const_made, 1)

            def tile(t, par, first):
                pool.wait_ge(var_ready, t + 1)
                if not first:
                    pool.wait_ge(fin_ready, t - 1)
                pool.tensor_tensor(rstd[:, par:par + 1], var[:, par:par + 1], half[:, 0:1], ALU.pow).then_inc(rstd_ready, 1)

            tile(0, 0, True)
            tile(1, 1, True)
            with pool.Fori(1, NT // 2) as tt:
                tile(2 * tt, 0, False)
                tile(2 * tt + 1, 1, False)


_INS = ["x", "adj", "L0_gnn_W_seq", "L0_gnn_a1", "L0_gnn_a2", "L0_gnn_W_out", "L0_gnn_b_out"]


def kernel(**inputs):
    import numpy as np
    import concourse.bacc as bacc
    from concourse.bass_utils import run_bass_kernel_spmd

    nc = bacc.Bacc("TRN2", target_bir_lowering=False, num_devices=1)
    arrays, args = {}, []
    for name in _INS:
        a = np.ascontiguousarray(inputs[name])
        arrays[f"in_{name}_dram"] = a
        args.append(nc.dram_tensor(f"in_{name}_dram", a.shape, mybir.dt.from_np(a.dtype), kind="ExternalInput").ap())
    shape = inputs["x"].shape
    args.append(nc.dram_tensor("out_0_dram", shape, F32, kind="ExternalOutput").ap())
    gat_layer(nc, *args)
    r = run_bass_kernel_spmd(nc, [arrays], core_ids=[0])
    return r.results[0]["out_0_dram"]
```

```python
from contextlib import ExitStack

import concourse.bass as bass
from concourse import mybir

ALU = mybir.AluOpType
ACT = mybir.ActivationFunctionType
AX = mybir.AxisListType
F32 = mybir.dt.float32
BF16 = mybir.dt.bfloat16
U32 = mybir.dt.uint32
I32 = mybir.dt.int32

P = 128
HEADS = 16
ALPHA = 0.2
EPS = 1e-5
QUARTERS = 4
SLOTS = 24
HARD = SLOTS + 1
GROUP = 4
UNIT = 32
NOWHERE = 1.0e6

R_IDX, R_VALID, R_A, R_C, R_SELF, R_LONE, R_ALL = 0, SLOTS, 2 * SLOTS, 2 * SLOTS + HEADS, 2 * SLOTS + 2 * HEADS, 2 * SLOTS + 2 * HEADS + 1, 96


def gat_layer(nc, x, adj, w_seq, a1, a2, w_out, b_out, out):
    N, D = x.shape
    NT = N // P
    KT = D // P
    SEQ = D + 2 * HEADS
    ROW = D + HEADS

    seq_d = nc.dram_tensor("seq_scratch", (N, SEQ), F32).ap()
    rec_d = nc.dram_tensor("record_scratch", (N, R_ALL), F32).ap()
    hid_d = nc.dram_tensor("hidden_scratch", (N, ROW), F32).ap()

    outer = ExitStack()
    with outer:
        def keep(name, shape, dt):
            return outer.enter_context(nc.sbuf_tensor(name, shape, dt))

        identf = keep("identf", [P, P], F32)
        identb = keep("identb", [P, P], BF16)
        ones = keep("ones", [P, P], F32)
        slots = keep("slots", [P, NT, SLOTS], F32)
        degree = keep("degree", [P, NT], F32)
        powers = keep("powers", [P, NT, 2, HEADS], F32)
        ctrl = keep("ctrl", [1, 2 * NT + 2], I32)

        project_and_search(nc, x, adj, w_seq, a1, a2, seq_d, identf, identb, ones, slots, degree, N, D, NT, KT, SEQ)
        sort_rows(nc, seq_d, rec_d, identf, ones, slots, degree, powers, ctrl, N, D, NT, SEQ)
        easy_rows(nc, seq_d, rec_d, hid_d, identf, identb, ctrl, N, D, NT, SEQ, ROW)
        hard_rows(nc, adj, seq_d, rec_d, hid_d, identf, ones, powers, ctrl, N, D, NT, ROW)
        output_layer(nc, x, w_out, b_out, rec_d, hid_d, out, identf, N, D, NT, KT, ROW)


def project_and_search(nc, x, adj, w_seq, a1, a2, seq_d, identf, identb, ones, slots, degree, N, D, NT, KT, SEQ):
    DH = D // HEADS
    SC = SEQ // 3
    QN = N // QUARTERS
    with ExitStack() as ctx:
        def sb(name, shape, dt):
            return ctx.enter_context(nc.sbuf_tensor(name, shape, dt))

        def ps(name, shape, dt):
            return ctx.enter_context(nc.psum_tensor(name, shape, dt))

        def sem(name):
            return ctx.enter_context(nc.semaphore(name))

        w = sb("w", [P, KT, SEQ], F32)
        avec = sb("avec", [P, 2, DH], F32)
        wa_tmp = sb("wa_tmp", [P, HEADS, DH], F32)
        xin = sb("xin", [P, 2, D], F32)
        xT = sb("xT", [P, 2, KT, P], F32)
        adj_in = sb("adj_in", [P, 2, N], F32)
        number = sb("number", [P, N], F32)
        numbered = sb("numbered", [P, N], F32)
        unused = sb("unused", [P, N], BF16)
        row_sum = sb("row_sum", [P, 2], F32)
        cand = sb("cand", [P, 3, 8 * QUARTERS], F32)
        found = sb("found", [P, SLOTS], F32)
        seq = sb("seq", [P, 2, SEQ], F32)
        xT_ps = ps("xT_ps", [P, 2, KT // 2, P], F32)
        seq_ps = ps("seq_ps", [P, 2, 3, 512], F32)

        ident_made = sem("ident_made")
        number_made = sem("number_made")
        w_in = sem("w_in")
        a_in = sem("a_in")
        wa_mul = sem("wa_mul")
        wa_sum = sem("wa_sum")
        x_in = [sem("x_in0"), sem("x_in1")]
        adj_arrived = [sem("adj_in0"), sem("adj_in1")]
        x_turned = sem("x_turned")
        xT_copied = sem("xT_copied")
        summed = sem("summed")
        is_numbered = sem("is_numbered")
        kept = sem("kept")
        seq_done = sem("seq_done")
        seq_copied = sem("seq_copied")
        seq_out = [sem("seq_out0"), sem("seq_out1")]

        block = ctx.enter_context(nc.Block())

        @block.gpsimd
        def _(pool):
            pool.memset(identf[:, :], 0.0).then_inc(ident_made, 1)
            pool.memset(identb[:, :], 0.0).then_inc(ident_made, 1)
            pool.memset(ones[:, :], 1.0).then_inc(ident_made, 1)
            pool.wait_ge(ident_made, 3)
            for m in (identf, identb):
                pool.affine_select(out=m[:, :], in_=m[:, :], compare_op=ALU.not_equal, fill=1.0,
                                   base=0, pattern=[[-1, P]], channel_multiplier=1).then_inc(ident_made, 1)
            pool.iota(numbered[:, :].bitcast(I32), pattern=[[1, N]], base=1, channel_multiplier=0).then_inc(number_made, 1)
            pool.wait_ge(number_made, 1)
            pool.tensor_copy(number[:, :], numbered[:, :].bitcast(I32)).then_inc(number_made, 1)

        @block.sync
        def _(sp):
            sp.dma_start(avec[:, 0, :], a2.partition_broadcast(P)).then_inc(a_in, 16)
            sp.dma_start(avec[:, 1, :], a1.partition_broadcast(P)).then_inc(a_in, 16)

            def loads(t, par, first):
                if not first:
                    sp.wait_ge(x_turned, t - 1)
                sp.dma_start(xin[:, par, :], x[bass.ds(t * P, P), :]).then_inc(x_in[par], 16)
                if not first:
                    sp.wait_ge(is_numbered, t - 1)
                    sp.wait_ge(summed, t - 1)
                sp.dma_start(adj_in[:, par, :], adj[bass.ds(t * P, P), :]).then_inc(adj_arrived[par], 16)

            for k in range(KT):
                sp.dma_start(w[:, k, 0:D], w_seq[k * P:(k + 1) * P, :]).then_inc(w_in, 16)
                if k == 0:
                    loads(0, 0, True)
            loads(1, 1, True)
            with sp.Fori(1, NT // 2) as tt:
                loads(2 * tt, 0, False)
                loads(2 * tt + 1, 1, False)

        @block.tensor
        def _(pe):
            pe.wait_ge(ident_made, 5)

            def turn(t, tt, par, very_first):
                pe.wait_ge(x_in[par], 16 * (tt + 1))
                if not very_first:
                    pe.wait_ge(xT_copied, t)
                for k in range(KT):
                    mm = pe.transpose(xT_ps[:, k // (KT // 2), k % (KT // 2), :], xin[:, par, k * P:(k + 1) * P],
                                      identf[:, :])
                mm.then_inc(x_turned, 1)

            def project(t, par, first):
                if not first:
                    pe.wait_ge(seq_copied, t - 1)
                pe.wait_ge(xT_copied, t + 1)
                for k in range(KT):
                    for c in range(3):
                        mm = pe.matmul(seq_ps[:, par, c, 0:SC], xT[:, par, k, :], w[:, k, c * SC:(c + 1) * SC],
                                       start=(k == 0), stop=(k == KT - 1))
                mm.then_inc(seq_done, 1)

            turn(0, 0, 0, True)
            turn(1, 0, 1, False)
            pe.wait_ge(w_in, 16 * KT)
            pe.wait_ge(wa_sum, 2 * KT)
            project(0, 0, True)
            turn(2, 1, 0, False)
            project(1, 1, True)
            turn(3, 1, 1, False)
            project(2, 0, False)
            with pe.Fori(2, NT // 2) as tt:
                turn(2 * tt, tt, 0, False)
                project(2 * tt - 1, 1, False)
                turn(2 * tt + 1, tt, 1, False)
                project(2 * tt, 0, False)
            project(NT - 1, 1, False)

        @block.vector
        def _(dve):
            dve.wait_ge(a_in, 32)
            n = 0
            dve.wait_ge(w_in, 16 * KT)
            for k in range(KT):
                for s in range(2):
                    if n:
                        dve.wait_ge(wa_sum, n)
                    dve.tensor_tensor(wa_tmp[:, :, :], w[:, k, 0:D].rearrange("p (h d) -> p h d", h=HEADS),
                                      avec[:, s:s + 1, :].broadcast_to([P, HEADS, DH]), ALU.mult).then_inc(wa_mul, 1)
                    n += 1
                    dve.wait_ge(wa_mul, n)
                    dve.tensor_reduce(w[:, k, D + s * HEADS:D + (s + 1) * HEADS], wa_tmp[:, :, :],
                                      AX.X, ALU.add).then_inc(wa_sum, 1)

            def copy_xT(t, par, first):
                dve.wait_ge(x_turned, t + 1)
                if not first:
                    dve.wait_ge(seq_done, t - 1)
                dve.tensor_copy(xT[:, par, :, :].rearrange("p (b k) i -> p b k i", b=2), xT_ps[:, :, :, :]).then_inc(xT_copied, 1)

            def search(t, tt, par):
                dve.wait_ge(adj_arrived[par], 16 * (tt + 1))
                dve.tensor_tensor(numbered[:, :], adj_in[:, par, :], number[:, :], ALU.mult).then_inc(is_numbered, 1)
                dve.drain()
                for q in range(QUARTERS):
                    dve.max(cand[:, 0, 8 * q:8 * (q + 1)], numbered[:, q * QN:(q + 1) * QN])
                dve.drain()
                for r in range(SLOTS // 8):
                    dve.max(found[:, 8 * r:8 * (r + 1)], cand[:, r, :])
                    dve.drain()
                    if r < SLOTS // 8 - 1:
                        dve.match_replace(cand[:, r + 1, :], found[:, 8 * r:8 * (r + 1)], cand[:, r, :], 0.0)
                        dve.drain()
                dve.tensor_copy(slots[:, bass.ds(t, 1), :], found[:, :].rearrange("p (o s) -> p o s", o=1))
                dve.wait_ge(summed, t + 1)
                dve.tensor_copy(degree[:, bass.ds(t, 1)], row_sum[:, par:par + 1]).then_inc(kept, 1)
                dve.drain()

            dve.wait_ge(number_made, 2)
            copy_xT(0, 0, True)
            copy_xT(1, 1, True)
            search(0, 0, 0)
            copy_xT(2, 0, False)
            search(1, 0, 1)
            with dve.Fori(1, NT // 2 - 1) as tt:
                copy_xT(2 * tt + 1, 1, False)
                search(2 * tt, tt, 0)
                copy_xT(2 * tt + 2, 0, False)
                search(2 * tt + 1, tt, 1)
            copy_xT(NT - 1, 1, False)
            search(NT - 2, NT // 2 - 1, 0)
            search(NT - 1, NT // 2 - 1, 1)

        @block.scalar
        def _(act):
            def add_up(t, tt, par, first, very_first):
                act.wait_ge(adj_arrived[par], 16 * (tt + 1))
                if not first:
                    act.wait_ge(kept, t - 1)
                if not very_first:
                    act.wait_ge(summed, t)
                act.activation(unused[:, :], adj_in[:, par, :], ACT.Copy,
                               accum_out=row_sum[:, par:par + 1]).then_inc(summed, 1)

            def evacuate(t, tt, par, first):
                act.wait_ge(seq_done, t + 1)
                if not first:
                    act.wait_ge(seq_out[par], 16 * tt)
                act.copy(seq[:, par, :].rearrange("p (c s) -> p c s", c=3), seq_ps[:, par, :, 0:SC]).then_inc(seq_copied, 1)
                act.wait_ge(seq_copied, t + 1)
                act.dma_start(seq_d[bass.ds(t * P, P), :], seq[:, par, :]).then_inc(seq_out[par], 16)

            add_up(0, 0, 0, True, True)
            add_up(1, 0, 1, True, False)
            evacuate(0, 0, 0, True)
            add_up(2, 1, 0, False, False)
            evacuate(1, 0, 1, True)
            add_up(3, 1, 1, False, False)
            evacuate(2, 1, 0, False)
            with act.Fori(2, NT // 2) as tt:
                add_up(2 * tt, tt, 0, False, False)
                evacuate(2 * tt - 1, tt - 1, 1, False)
                add_up(2 * tt + 1, tt, 1, False, False)
                evacuate(2 * tt, tt, 0, False)
            evacuate(NT - 1, NT // 2 - 1, 1, False)
            for par in range(2):
                act.wait_ge(seq_out[par], 16 * (NT // 2))


def sort_rows(nc, seq_d, rec_d, identf, ones, slots, degree, powers, ctrl, N, D, NT, SEQ):
    KEYS = HARD
    KC = KEYS * NT
    HC = KC // 2
    UNITS = N // UNIT
    with ExitStack() as ctx:
        def sb(name, shape, dt):
            return ctx.enter_context(nc.sbuf_tensor(name, shape, dt))

        def ps(name, shape, dt):
            return ctx.enter_context(nc.psum_tensor(name, shape, dt))

        def sem(name):
            return ctx.enter_context(nc.semaphore(name))

        scores = sb("scores", [P, NT, 2, HEADS], F32)
        part_max = sb("part_max", [P, HEADS], F32)
        head_max = sb("head_max", [HEADS, 1], F32)
        diag_max = sb("diag_max", [HEADS, HEADS], F32)
        max_s2 = sb("max_s2", [P, HEADS], F32)
        shifted = sb("shifted", [P, NT, HEADS], F32)
        bound = sb("bound", [P, NT, HEADS], F32)
        expo = sb("expo", [P, NT, 2, HEADS], F32)
        record = sb("record", [P, NT, R_ALL], F32)
        self_i = sb("self_i", [P, NT], I32)
        keys_i = sb("keys_i", [P, KEYS], I32)
        keys = sb("keys", [P, KEYS], F32)
        last_i = sb("last_i", [1, NT], I32)
        last = sb("last", [1, NT], F32)
        units_i = sb("units_i", [1, UNITS], I32)
        units = sb("units", [1, UNITS], F32)
        before = sb("before", [P, P], BF16)
        all_b = sb("all_b", [P, P], BF16)
        empty = sb("empty", [P, NT, SLOTS], F32)
        captured = sb("captured", [P, NT], F32)
        complete = sb("complete", [P, NT], F32)
        easy = sb("easy", [P, NT], F32)
        key = sb("key", [P, NT], F32)
        hot = sb("hot", [P, KEYS, NT], BF16)
        scan = sb("scan", [P, 2, KC], F32)
        total = sb("total", [P, KC], F32)
        place = sb("place", [P, KEYS, NT], F32)
        rank = sb("rank", [P, NT], F32)
        rank_u = sb("rank_u", [P, NT], U32)
        clipped = sb("clipped", [1, NT], F32)
        groups = sb("groups", [1, 2, NT], F32)
        starts = sb("starts", [1, 2, NT], F32)
        n_hard = sb("n_hard", [1, 1], F32)
        unit_on = sb("unit_on", [1, UNITS], F32)
        n_units = sb("n_units", [1, 1], F32)
        small_ps = ps("small_ps", [P, P], F32)
        max_ps = ps("max_ps", [P, HEADS], F32)
        pre_ps = ps("pre_ps", [P, 2, 512], F32)
        tot_ps = ps("tot_ps", [P, 2, 512], F32)

        scores_in = sem("scores_in")
        consts = sem("consts")
        step = sem("step")
        max_turned = sem("max_turned")
        max_spread = sem("max_spread")
        counted = sem("counted")
        exp_done = sem("exp_done")
        powers_out = sem("powers_out")
        ranked = sem("ranked")
        scattered = sem("scattered")

        block = ctx.enter_context(nc.Block())
        seq_v = seq_d.rearrange("(t p) c -> p t c", p=P)
        marks = {}

        @block.gpsimd
        def _(pool):
            pool.iota(self_i[:, :], pattern=[[P, NT]], base=0, channel_multiplier=1).then_inc(consts, 1)
            pool.iota(keys_i[:, :], pattern=[[1, KEYS]], base=1, channel_multiplier=0).then_inc(consts, 1)
            pool.iota(last_i[:, :], pattern=[[P, NT]], base=P - 1, channel_multiplier=0).then_inc(consts, 1)
            pool.iota(units_i[:, :], pattern=[[UNIT, UNITS]], base=0, channel_multiplier=0).then_inc(consts, 1)
            pool.memset(all_b[:, :], 1.0).then_inc(consts, 1)
            pool.memset(record[:, :, R_LONE:R_ALL], 0.0).then_inc(consts, 1)
            pool.wait_ge(consts, 6)
            pool.affine_select(out=before[:, :], in_=all_b[:, :], compare_op=ALU.is_gt, fill=0.0,
                               base=0, pattern=[[1, P]], channel_multiplier=-1).then_inc(consts, 1)
            pool.wait_ge(ranked, 1)
            pool.wait_ge(exp_done, 3)
            for t in range(NT):
                pool.indirect_dma_start(rec_d, bass.IndirectOffsetOnAxis(ap=rank_u[:, t:t + 1], axis=0),
                                        record[:, t, :], None, bounds_check=N - 1).then_inc(scattered, 16)
            pool.wait_ge(scattered, 16 * NT)

        @block.sync
        def _(sp):
            sp.dma_start(scores[:, :, :, :].rearrange("p t s h -> p t (s h)"), seq_v[:, :, D:SEQ]).then_inc(scores_in, 16)
            sp.wait_ge(exp_done, 2)
            sp.dma_start(seq_v[:, :, D:SEQ], powers[:, :, :, :].rearrange("p t s h -> p t (s h)")).then_inc(powers_out, 16)
            sp.wait_ge(powers_out, 16)

        @block.vector
        def _(dve):
            n = 0

            def done(ins, name=None):
                nonlocal n
                ins.then_inc(step, 1)
                n += 1
                if name:
                    marks[name] = n

            s2 = scores[:, :, 0, :]
            s1 = scores[:, :, 1, :]
            dve.wait_ge(consts, 7)
            done(dve.tensor_scalar(record[:, :, R_VALID:R_A], slots[:, :, :], 0.0, None, ALU.is_gt))
            done(dve.tensor_scalar(empty[:, :, :], slots[:, :, :], 0.0, NOWHERE, ALU.is_equal, ALU.mult))
            done(dve.tensor_copy(keys[:, :], keys_i[:, :]))
            done(dve.tensor_copy(last[:, :], last_i[:, :]))
            done(dve.tensor_copy(units[:, :], units_i[:, :]))
            dve.wait_ge(step, n)
            done(dve.tensor_reduce(captured[:, :], record[:, :, R_VALID:R_A], AX.X, ALU.add))
            done(dve.scalar_tensor_tensor(record[:, :, R_IDX:R_VALID].bitcast(U32), slots[:, :, :], -1.0,
                                          empty[:, :, :], ALU.add, ALU.add))
            dve.wait_ge(step, n)
            done(dve.tensor_tensor(complete[:, :], captured[:, :], degree[:, :], ALU.is_equal))
            dve.wait_ge(step, n)
            done(dve.scalar_tensor_tensor(easy[:, :], degree[:, :], 0.0, complete[:, :], ALU.is_gt, ALU.mult))
            dve.wait_ge(step, n)
            done(dve.scalar_tensor_tensor(key[:, :], degree[:, :], -float(HARD), easy[:, :], ALU.add, ALU.mult))
            dve.wait_ge(step, n)
            done(dve.tensor_scalar(keys[:, :], keys[:, :], -float(HARD), None, ALU.add))
            dve.wait_ge(step, n)
            done(dve.tensor_tensor(hot[:, :, :], key[:, None, :].broadcast_to([P, KEYS, NT]),
                                   keys[:, :, None].broadcast_to([P, KEYS, NT]), ALU.is_equal), "hot")
            done(dve.tensor_copy(record[:, :, R_SELF].bitcast(U32), self_i[:, :]))
            done(dve.tensor_scalar(record[:, :, R_LONE], degree[:, :], 0.0, None, ALU.is_equal))
            dve.wait_ge(scores_in, 16)
            done(dve.tensor_reduce(part_max[:, :], s2.rearrange("p t h -> p h t"), AX.X, ALU.max), "part_max")
            dve.wait_ge(max_turned, 1)
            done(dve.tensor_reduce(head_max[:, :], small_ps[0:HEADS, :], AX.X, ALU.max))
            dve.wait_ge(step, n)
            done(dve.tensor_scalar(diag_max[:, :], identf[0:HEADS, 0:HEADS], head_max[:, 0:1], None, ALU.mult), "diag_max")
            dve.wait_ge(max_spread, 1)
            done(dve.tensor_copy(max_s2[:, :], max_ps[:, :]))
            dve.wait_ge(step, n)
            m = max_s2[:, None, :].broadcast_to([P, NT, HEADS])
            done(dve.tensor_tensor(shifted[:, :, :], s2, m, ALU.subtract), "shifted")
            done(dve.tensor_tensor(bound[:, :, :], s1, m, ALU.add))
            dve.wait_ge(step, n)
            done(dve.tensor_scalar(expo[:, :, 0, :], bound[:, :, :], 0.0, 1.0 - ALPHA, ALU.min, ALU.mult))
            done(dve.tensor_scalar(expo[:, :, 1, :], bound[:, :, :], 0.0, ALPHA - 1.0, ALU.max, ALU.mult), "expo")
            dve.wait_ge(counted, 1)
            done(dve.tensor_copy(total[:, :].rearrange("p (b c) -> p b c", b=2), tot_ps[:, :, 0:HC]))
            dve.wait_ge(step, n)
            done(dve.tensor_copy(scan[:, 0, :], total[:, :]))
            cur, d = 0, 1
            while d < KC:
                dve.wait_ge(step, n)
                done(dve.tensor_tensor(scan[:, 1 - cur, d:KC], scan[:, cur, d:KC], scan[:, cur, 0:KC - d], ALU.add))
                done(dve.tensor_copy(scan[:, 1 - cur, 0:d], scan[:, cur, 0:d]))
                cur, d = 1 - cur, 2 * d
            dve.wait_ge(step, n)
            done(dve.tensor_tensor(scan[:, 1 - cur, :], scan[:, cur, :], total[:, :], ALU.subtract))
            first = scan[:, 1 - cur, :]
            dve.wait_ge(step, n)
            done(dve.tensor_tensor(total[:, :].rearrange("p (b c) -> p b c", b=2), pre_ps[:, :, 0:HC],
                                   first.rearrange("p (b c) -> p b c", b=2), ALU.add))
            dve.wait_ge(step, n)
            done(dve.tensor_tensor(place[:, :, :], total[:, :].rearrange("p (k t) -> p k t", k=KEYS), hot[:, :, :], ALU.mult))
            dve.wait_ge(step, n)
            done(dve.tensor_reduce(rank[:, :], place[:, :, :].rearrange("p k t -> p t k"), AX.X, ALU.add))
            dve.wait_ge(step, n)
            dve.tensor_copy(rank_u[:, :], rank[:, :]).then_inc(ranked, 1)
            row0 = scan[0:1, 1 - cur, :]
            hard0 = row0[:, (HARD - 1) * NT:(HARD - 1) * NT + 1]
            done(dve.tensor_scalar(n_hard[:, :], hard0, -1.0, float(N), ALU.mult, ALU.add))
            done(dve.tensor_scalar(clipped[:, :], hard0.broadcast_to([1, NT]), -1.0, None, ALU.add))
            dve.wait_ge(step, n)
            done(dve.tensor_tensor(clipped[:, :], clipped[:, :], last[:, :], ALU.min))
            done(dve.tensor_scalar(groups[:, 0, :], last[:, :], 0.0, None, ALU.mult))
            g = 0
            for k in range(0, SLOTS, GROUP):
                dve.wait_ge(step, n)
                done(dve.scalar_tensor_tensor(groups[:, 1 - g, :], clipped[:, :], row0[:, k * NT:k * NT + 1],
                                              groups[:, g, :], ALU.is_ge, ALU.add))
                g = 1 - g
            dve.wait_ge(step, n)
            done(dve.tensor_scalar(groups[:, 1 - g, :], groups[:, g, :], 1.0, None, ALU.max))
            g = 1 - g
            dve.wait_ge(step, n)
            done(dve.tensor_copy(starts[:, 0, :], groups[:, g, :]))
            cur, d = 0, 1
            while d < NT:
                dve.wait_ge(step, n)
                done(dve.tensor_tensor(starts[:, 1 - cur, d:NT], starts[:, cur, d:NT], starts[:, cur, 0:NT - d], ALU.add))
                done(dve.tensor_copy(starts[:, 1 - cur, 0:d], starts[:, cur, 0:d]))
                cur, d = 1 - cur, 2 * d
            dve.wait_ge(step, n)
            done(dve.tensor_copy(ctrl[:, 0:NT], groups[:, g, :]))
            done(dve.tensor_tensor(ctrl[:, NT:2 * NT], starts[:, cur, :], groups[:, g, :], ALU.subtract))
            done(dve.tensor_scalar(unit_on[:, :], units[:, :], n_hard[:, 0:1], None, ALU.is_lt))
            dve.wait_ge(step, n)
            done(dve.tensor_reduce(n_units[:, :], unit_on[:, :], AX.X, ALU.add))
            dve.wait_ge(step, n)
            done(dve.tensor_scalar(ctrl[:, 2 * NT:2 * NT + 1], n_units[:, :], 1.0, None, ALU.max))

        @block.tensor
        def _(pe):
            pe.wait_ge(step, marks["hot"])
            for b in range(2):
                flat = hot[:, :, :].rearrange("p k t -> p (k t)")[:, b * HC:(b + 1) * HC]
                pe.matmul(pre_ps[:, b, 0:HC], before[:, :], flat, start=True, stop=True)
                mm = pe.matmul(tot_ps[:, b, 0:HC], all_b[:, :], flat, start=True, stop=True)
            mm.then_inc(counted, 1)
            pe.wait_ge(step, marks["part_max"])
            pe.transpose(small_ps[0:HEADS, :], part_max[:, :], identf[:, :]).then_inc(max_turned, 1)
            pe.wait_ge(step, marks["diag_max"])
            pe.matmul(max_ps[:, :], ones[0:HEADS, :], diag_max[:, :], start=True, stop=True).then_inc(max_spread, 1)

        @block.scalar
        def _(act):
            act.wait_ge(step, marks["shifted"])
            act.activation(powers[:, :, 0, :], shifted[:, :, :], ACT.Exp).then_inc(exp_done, 1)
            act.activation(powers[:, :, 1, :], shifted[:, :, :], ACT.Exp, scale=ALPHA).then_inc(exp_done, 1)
            act.wait_ge(step, marks["expo"])
            act.activation(record[:, :, R_A:R_SELF].rearrange("p t (s h) -> p t s h", s=2), expo[:, :, :, :],
                           ACT.Exp).then_inc(exp_done, 1)


def easy_rows(nc, seq_d, rec_d, hid_d, identf, identb, ctrl, N, D, NT, SEQ, ROW):
    DH = D // HEADS
    MOST = SLOTS // GROUP
    with ExitStack() as ctx:
        def sb(name, shape, dt):
            return ctx.enter_context(nc.sbuf_tensor(name, shape, dt))

        def sem(name):
            return ctx.enter_context(nc.semaphore(name))

        rec = sb("rec", [P, 2, R_ALL], F32)
        index = sb("index", [P, GROUP], U32)
        near = sb("near", [P, GROUP, SEQ], F32)
        both = sb("both", [P, GROUP, 2, HEADS], F32)
        prod = sb("prod", [P, GROUP, ROW], F32)
        zero = sb("zero", [P, 512], BF16)
        sums = sb("sums", [P, 2, ROW], F32)
        acc = ctx.enter_context(nc.psum_tensor("acc", [P, 2, 3, 512], F32))

        rec_in = [sem("rec_in0"), sem("rec_in1")]
        index_ready = sem("index_ready")
        near_in = [sem(f"near_in{s}") for s in range(GROUP)]
        near_done = sem("near_done")
        both_ready = sem("both_ready")
        weight_ready = sem("weight_ready")
        prod_free = sem("prod_free")
        zero_made = sem("zero_made")
        carried = sem("carried")
        acc_done = sem("acc_done")
        acc_copied = sem("acc_copied")
        sums_out = [sem("sums_out0"), sem("sums_out1")]

        block = ctx.enter_context(nc.Block())

        def tiles(eng, tile):
            tile(0, 0, 0, True)
            tile(1, 0, 1, True)
            with eng.Fori(1, NT // 2) as tt:
                tile(2 * tt, tt, 0, False)
                tile(2 * tt + 1, tt, 1, False)

        def extent(eng, t):
            return (eng.value_load(ctrl[0:1, bass.ds(t, 1)], min_val=1, max_val=MOST),
                    eng.value_load(ctrl[0:1, bass.ds(t + NT, 1)], min_val=0, max_val=MOST * NT))

        @block.sync
        def _(sp):
            def tile(t, tt, par, first):
                if not first:
                    sp.wait_ge(acc_copied, t - 1)
                sp.dma_start(rec[:, par, :], rec_d[bass.ds(t * P, P), :]).then_inc(rec_in[par], 16)
            tiles(sp, tile)

        @block.gpsimd
        def _(pool):
            def tile(t, tt, par, first):
                count, start = extent(pool, t)
                pool.wait_ge(rec_in[par], 16 * (tt + 1))
                pool.sem_inc(carried, 1)
                with pool.Fori(0, count) as u:
                    for s in range(GROUP):
                        n = (start + u) * GROUP + s
                        pool.wait_ge(near_done, n + 1)
                        pool.tensor_copy(index[:, s:s + 1], rec[:, par, bass.ds(u * GROUP + (R_IDX + s), 1)].bitcast(U32)
                                         ).then_inc(index_ready, 1)
                        pool.wait_ge(index_ready, n + 1)
                        pool.sem_inc(carried, 1)
                        pool.indirect_dma_start(near[:, s, :], None, seq_d,
                                                bass.IndirectOffsetOnAxis(ap=index[:, s:s + 1], axis=0),
                                                bounds_check=N - 1, oob_is_err=False).then_inc(near_in[s], 16)
            tiles(pool, tile)

        @block.vector
        def _(dve):
            dve.memset(zero[:, :], 0.0).then_inc(zero_made, 1)
            for s in range(GROUP):
                dve.memset(near[:, s, :], 0.0).then_inc(near_done, 1)
                dve.memset(prod[:, s, 0:1], 0.0).then_inc(prod_free, 1)
            dve.wait_ge(near_done, GROUP)
            dve.wait_ge(prod_free, GROUP)

            def tile(t, tt, par, first):
                count, start = extent(dve, t)
                dve.wait_ge(rec_in[par], 16 * (tt + 1))
                dve.sem_inc(carried, 1)
                with dve.Fori(0, count) as u:
                    for s in range(GROUP):
                        n = (start + u) * GROUP + s
                        dve.wait_ge(near_in[s], (start + u + 1) * 16)
                        dve.scalar_tensor_tensor(both[:, s, :, :].rearrange("p a h -> p (a h)"), near[:, s, D:SEQ],
                                                 rec[:, par, bass.ds(u * GROUP + (R_VALID + s), 1)],
                                                 rec[:, par, R_A:R_SELF], ALU.mult, ALU.mult).then_inc(both_ready, 1)
                        dve.wait_ge(prod_free, n + 1)
                        dve.wait_ge(both_ready, n + 1)
                        dve.tensor_tensor(prod[:, s, D:ROW], both[:, s, 0, :], both[:, s, 1, :], ALU.max).then_inc(weight_ready, 1)
                        dve.wait_ge(weight_ready, n + 1)
                        dve.tensor_tensor(prod[:, s, 0:D].rearrange("p (h d) -> p h d", h=HEADS),
                                          near[:, s, 0:D].rearrange("p (h d) -> p h d", h=HEADS),
                                          prod[:, s, D:ROW].rearrange("p (h o) -> p h o", o=1).broadcast_to([P, HEADS, DH]),
                                          ALU.mult).then_inc(near_done, 1)
            tiles(dve, tile)

        @block.tensor
        def _(pe):
            pe.wait_ge(zero_made, 1)

            def tile(t, tt, par, first):
                count, start = extent(pe, t)
                if not first:
                    pe.wait_ge(acc_copied, t - 1)
                for c, m in enumerate((512, 512, HEADS)):
                    pe.matmul(acc[:, par, c, 0:m], identb[:, :], zero[:, 0:m], start=True, stop=False, skip_group_check=True)
                with pe.Fori(0, count) as u:
                    for s in range(GROUP):
                        n = (start + u) * GROUP + s
                        pe.wait_ge(near_done, n + 1 + GROUP)
                        for c, m in enumerate((512, 512, HEADS)):
                            mm = pe.matmul(acc[:, par, c, 0:m], identf[:, :], prod[:, s, c * 512:c * 512 + m],
                                           start=False, stop=False, skip_group_check=True)
                        mm.then_inc(prod_free, 1)
                pe.matmul(acc[:, par, 2, 0:HEADS], identb[:, :], zero[:, 0:HEADS], start=False, stop=True,
                          skip_group_check=True).then_inc(acc_done, 1)
            tiles(pe, tile)

        @block.scalar
        def _(act):
            def tile(t, tt, par, first):
                act.wait_ge(acc_done, t + 1)
                if not first:
                    act.wait_ge(sums_out[par], 16 * tt)
                act.copy(sums[:, par, 0:D].rearrange("p (c f) -> p c f", c=2), acc[:, par, 0:2, :])
                act.copy(sums[:, par, D:ROW], acc[:, par, 2, 0:HEADS]).then_inc(acc_copied, 1)
                act.wait_ge(acc_copied, t + 1)
                act.dma_start(hid_d[bass.ds(t * P, P), :], sums[:, par, :]).then_inc(sums_out[par], 16)
            tiles(act, tile)
            for par in range(2):
                act.wait_ge(sums_out[par], 16 * (NT // 2))


def hard_rows(nc, adj, seq_d, rec_d, hid_d, identf, ones, powers, ctrl, N, D, NT, ROW):
    DH = D // HEADS
    with ExitStack() as ctx:
        def sb(name, shape, dt):
            return ctx.enter_context(nc.sbuf_tensor(name, shape, dt))

        def ps(name, shape, dt):
            return ctx.enter_context(nc.psum_tensor(name, shape, dt))

        def sem(name):
            return ctx.enter_context(nc.semaphore(name))

        urec = sb("urec", [UNIT, R_ALL], F32)
        uadj = sb("uadj", [UNIT, N], F32)
        uadjT = sb("uadjT", [P, NT, UNIT], F32)
        diag = sb("diag", [UNIT, 2, HEADS, UNIT], F32)
        factor = sb("factor", [P, 2, HEADS, UNIT], F32)
        values = sb("values", [P, 2, NT, DH + 1], F32)
        pos = sb("pos_w", [P, NT, UNIT], F32)
        neg = sb("neg_w", [P, NT, UNIT], F32)
        weight = sb("weight", [P, 2, NT, UNIT], F32)
        uhid = sb("uhid", [UNIT, ROW], F32)
        adjT_ps = ps("uadjT_ps", [P, 2, NT // 2, UNIT], F32)
        factor_ps = ps("factor_ps", [P, 2, HEADS * UNIT], F32)
        head_ps = ps("head_ps", [UNIT, 2, 512], F32)

        ones_made = sem("ones_made")
        urec_in = sem("urec_in")
        uadj_in = sem("uadj_in")
        diag_ready = sem("diag_ready")
        lone_fixed = sem("lone_fixed")
        spread = sem("spread")
        turned = sem("turned")
        copied = sem("copied")
        values_in = [sem("values_in0"), sem("values_in1")]
        part_ready = sem("part_ready")
        weight_ready = sem("uweight_ready")
        head_done = sem("head_done")
        head_copied = sem("head_copied")
        unit_out = sem("unit_out")
        carried = sem("carried_u")

        block = ctx.enter_context(nc.Block())
        seq_v = seq_d.rearrange("(t p) c -> p t c", p=P)

        def number(eng):
            return eng.value_load(ctrl[0:1, 2 * NT:2 * NT + 1], min_val=1, max_val=N // UNIT)

        def first_row(d):
            return d * -UNIT + (N - UNIT)

        @block.sync
        def _(sp):
            count = number(sp)
            sp.wait_ge(ones_made, 1)
            with sp.Fori(0, count) as d:
                sp.dma_start(urec[:, :], rec_d[bass.ds(first_row(d), UNIT), :]).then_inc(urec_in, 16)

                def load(h, hp):
                    sp.dma_start(values[:, hp, :, 0:DH], seq_v[:, :, bass.ds(h * DH, DH)]).then_inc(values_in[hp], 16)

                load(0, 0)
                load(1, 1)
                with sp.Fori(1, HEADS // 2) as hh:
                    for hp in range(2):
                        sp.wait_ge(head_done, d * HEADS + (2 * hh + (hp - 1)))
                        load(2 * hh + hp, hp)
                sp.wait_ge(head_copied, (d + 1) * (2 * HEADS))
                sp.sem_inc(carried, 1)
                sp.dma_start(hid_d[bass.ds(first_row(d), UNIT), :], uhid[:, :]).then_inc(unit_out, 16)
                sp.wait_ge(unit_out, (d + 1) * 16)
                sp.sem_inc(carried, 1)

        @block.gpsimd
        def _(pool):
            count = number(pool)
            pool.memset(values[:, :, :, DH:DH + 1], 1.0).then_inc(ones_made, 1)
            with pool.Fori(0, count) as d:
                pool.wait_ge(urec_in, (d + 1) * 16)
                pool.sem_inc(carried, 1)
                pool.indirect_dma_start(uadj[:, :], None, adj,
                                        bass.IndirectOffsetOnAxis(ap=urec[:, R_SELF:R_SELF + 1].bitcast(U32), axis=0),
                                        bounds_check=N - 1).then_inc(uadj_in, 16)

        @block.vector
        def _(dve):
            count = number(dve)
            with dve.Fori(0, count) as d:
                dve.wait_ge(urec_in, (d + 1) * 16)
                for s, col in enumerate((R_A, R_C)):
                    dve.tensor_tensor(diag[:, s, :, :],
                                      urec[:, col:col + HEADS].rearrange("p (h o) -> p h o", o=1).broadcast_to([UNIT, HEADS, UNIT]),
                                      identf[0:UNIT, 0:UNIT].rearrange("p (o i) -> p o i", o=1).broadcast_to([UNIT, HEADS, UNIT]),
                                      ALU.mult).then_inc(diag_ready, 1)
                dve.wait_ge(uadj_in, (d + 1) * 16)
                dve.tensor_scalar(uadj[:, :], uadj[:, :], urec[:, R_LONE:R_LONE + 1], None, ALU.max).then_inc(lone_fixed, 1)
                dve.wait_ge(spread, d + 1)
                dve.tensor_copy(factor[:, :, :, :].rearrange("p s h i -> p s (h i)"), factor_ps[:, :, :]).then_inc(copied, 1)
                dve.wait_ge(turned, d + 1)
                dve.tensor_copy(uadjT[:, :, :].rearrange("p (b j) i -> p b j i", b=2), adjT_ps[:, :, :, :]).then_inc(copied, 1)
                dve.wait_ge(copied, d * 2 + 2)

                def head(h, hp, first):
                    n = d * (3 * HEADS) + h * 3
                    for out, s in ((pos, 0), (neg, 1)):
                        dve.tensor_tensor(out[:, :, :], factor[:, s, bass.ds(h, 1), :].broadcast_to([P, NT, UNIT]),
                                          powers[:, :, s, bass.ds(h, 1)].broadcast_to([P, NT, UNIT]),
                                          ALU.mult).then_inc(part_ready, 1)
                    dve.wait_ge(part_ready, n + 2)
                    dve.tensor_tensor(pos[:, :, :], pos[:, :, :], neg[:, :, :], ALU.max).then_inc(part_ready, 1)
                    if not first:
                        dve.wait_ge(head_done, d * HEADS + (h - 1))
                    dve.wait_ge(part_ready, n + 3)
                    dve.tensor_tensor(weight[:, hp, :, :], pos[:, :, :], uadjT[:, :, :], ALU.mult).then_inc(weight_ready, 1)
                    dve.wait_ge(weight_ready, d * HEADS + (h + 1))
                    dve.sem_inc(carried, 1)

                head(0, 0, True)
                head(1, 1, True)
                with dve.Fori(1, HEADS // 2) as hh:
                    head(2 * hh, 0, False)
                    head(2 * hh + 1, 1, False)

        @block.tensor
        def _(pe):
            count = number(pe)
            with pe.Fori(0, count) as d:
                pe.wait_ge(diag_ready, d * 2 + 2)
                for s in range(2):
                    mm = pe.matmul(factor_ps[:, s, :], ones[0:UNIT, :], diag[:, s, :, :].rearrange("p h i -> p (h i)"),
                                   start=True, stop=True)
                mm.then_inc(spread, 1)
                pe.wait_ge(lone_fixed, d + 1)
                pe.sem_inc(carried, 1)
                for j in range(NT):
                    mm = pe.transpose(adjT_ps[:, j // (NT // 2), j % (NT // 2), :], uadj[:, j * P:(j + 1) * P],
                                      identf[0:UNIT, 0:UNIT])
                mm.then_inc(turned, 1)

                def head(h, hh, hp, first):
                    pe.wait_ge(values_in[hp], (d * (HEADS // 2) + (hh + 1)) * 16)
                    pe.wait_ge(weight_ready, d * HEADS + (h + 1))
                    if not first:
                        pe.wait_ge(head_copied, d * (2 * HEADS) + (h - 1) * 2)
                    for j in range(NT):
                        mm = pe.matmul(head_ps[:, hp, 0:DH + 1], weight[:, hp, j, :], values[:, hp, j, :],
                                       start=(j == 0), stop=(j == NT - 1))
                    mm.then_inc(head_done, 1)

                head(0, 0, 0, True)
                head(1, 0, 1, True)
                with pe.Fori(1, HEADS // 2) as hh:
                    head(2 * hh, hh, 0, False)
                    head(2 * hh + 1, hh, 1, False)

        @block.scalar
        def _(act):
            count = number(act)
            with act.Fori(0, count) as d:
                with act.Fori(0, HEADS // 2) as hh:
                    for hp in range(2):
                        h = 2 * hh + hp
                        act.wait_ge(head_done, d * HEADS + (h + 1))
                        act.copy(uhid[:, bass.ds(h * DH, DH)], head_ps[:, hp, 0:DH]).then_inc(head_copied, 1)
                        act.copy(uhid[:, bass.ds(h + D, 1)], head_ps[:, hp, DH:DH + 1]).then_inc(head_copied, 1)


def output_layer(nc, x, w_out, b_out, rec_d, hid_d, out, identf, N, D, NT, KT, ROW):
    DH = D // HEADS
    CH = D // 512
    with ExitStack() as ctx:
        def sb(name, shape, dt):
            return ctx.enter_context(nc.sbuf_tensor(name, shape, dt))

        def sem(name):
            return ctx.enter_context(nc.semaphore(name))

        w = sb("w_out_sb", [P, KT, D], F32)
        bias = sb("bias", [P, D], F32)
        hid = sb("hid", [P, 2, ROW], F32)
        recip = sb("recip", [P, 2, HEADS], F32)
        normed = sb("normed", [P, 2, D], F32)
        own = sb("own", [P, NT, R_ALL - R_SELF], U32)
        own_t = sb("own_t", [P, 2], U32)
        own_s = sb("own_s", [P, 2], U32)
        xin = sb("x_res", [P, 2, D], F32)
        hT = sb("hT", [P, 2, KT, P], F32)
        z = sb("z", [P, 2, D], F32)
        neg = sb("neg", [P, 2, D], F32)
        e = sb("e", [P, 2, D], F32)
        y = sb("y", [P, 2, D], F32)
        fin = sb("fin", [P, 2, D], F32)
        pos = sb("pos", [P, 2, D], F32)
        stats = sb("stats", [P, 2, CH, 6], F32)
        mv = sb("mv", [P, 2, 2], F32)
        var = sb("var", [P, 2], F32)
        rstd = sb("rstd", [P, 2], F32)
        hT_ps = ctx.enter_context(nc.psum_tensor("hT_ps", [P, KT, P], F32))
        z_ps = ctx.enter_context(nc.psum_tensor("z_ps", [P, 2, CH, 512], F32))

        half = sb("half", [P, 2], F32)
        w_in = sem("w_out_in")
        b_in = sem("b_in")
        const_made = sem("const_made")
        hid_in = [sem("hid_in0"), sem("hid_in1")]
        x_in = [sem("x_res0"), sem("x_res1")]
        own_in = sem("own_in")
        carried = sem("carried_o")
        own_ready = sem("own_ready")
        own_s_ready = sem("own_s_ready")
        recip_ready = sem("recip_ready")
        normalised = sem("normalised")
        h_turned = sem("h_turned")
        hT_copied = sem("hT_copied")
        z_done = sem("z_done")
        z_ready = sem("z_ready")
        neg_ready = sem("neg_ready")
        exp_ready = sem("exp_ready")
        pos_ready = sem("pos_ready")
        y_ready = sem("y_ready")
        stats_ready = sem("stats_ready")
        mv_ready = sem("mv_ready")
        var_ready = sem("var_ready")
        rstd_ready = sem("rstd_ready")
        fin_ready = sem("fin_ready")
        out_stored = [sem("out0"), sem("out1")]

        block = ctx.enter_context(nc.Block())

        @block.sync
        def _(sp):
            sp.dma_start(bias[:, :], b_out.partition_broadcast(P)).then_inc(b_in, 16)
            sp.dma_start(own[:, :, :], rec_d[:, R_SELF:R_ALL].bitcast(U32).rearrange("(t p) c -> p t c", p=P)).then_inc(own_in, 16)

            def load(t, par, first):
                if not first:
                    sp.wait_ge(normalised, t - 1)
                sp.dma_start(hid[:, par, :], hid_d[bass.ds(t * P, P), :]).then_inc(hid_in[par], 16)

            load(0, 0, True)
            load(1, 1, True)
            for k in range(KT):
                sp.dma_start(w[:, k, :], w_out[k * P:(k + 1) * P, :]).then_inc(w_in, 16)
            with sp.Fori(1, NT // 2) as tt:
                for par in range(2):
                    load(2 * tt + par, par, False)

        @block.tensor
        def _(pe):
            def turn(t, tt, par, very_first):
                pe.wait_ge(normalised, t + 1)
                if not very_first:
                    pe.wait_ge(hT_copied, t)
                for k in range(KT):
                    mm = pe.transpose(hT_ps[:, k, :], normed[:, par, k * P:(k + 1) * P], identf[:, :])
                mm.then_inc(h_turned, 1)

            def project(t, par, first):
                pe.wait_ge(hT_copied, t + 1)
                if not first:
                    pe.wait_ge(z_ready, t - 1)
                for k in range(KT):
                    for c in range(CH):
                        mm = pe.matmul(z_ps[:, par, c, :], hT[:, par, k, :], w[:, k, c * 512:(c + 1) * 512],
                                       start=(k == 0), stop=(k == KT - 1))
                mm.then_inc(z_done, 1)

            turn(0, 0, 0, True)
            pe.wait_ge(w_in, 16 * KT)
            turn(1, 0, 1, False)
            project(0, 0, True)
            turn(2, 1, 0, False)
            project(1, 1, True)
            turn(3, 1, 1, False)
            project(2, 0, False)
            with pe.Fori(2, NT // 2) as tt:
                turn(2 * tt, tt, 0, False)
                project(2 * tt - 1, 1, False)
                turn(2 * tt + 1, tt, 1, False)
                project(2 * tt, 0, False)
            project(NT - 1, 1, False)

        @block.vector
        def _(dve):
            def normalise(t, tt, par, first):
                dve.wait_ge(hid_in[par], 16 * (tt + 1))
                dve.reciprocal(recip[:, par, :], hid[:, par, D:ROW]).then_inc(recip_ready, 1)
                if not first:
                    dve.wait_ge(h_turned, t - 1)
                dve.wait_ge(recip_ready, t + 1)
                dve.tensor_tensor(normed[:, par, :].rearrange("p (h d) -> p h d", h=HEADS),
                                  hid[:, par, 0:D].rearrange("p (h d) -> p h d", h=HEADS),
                                  recip[:, par, :].rearrange("p (h o) -> p h o", o=1).broadcast_to([P, HEADS, DH]),
                                  ALU.mult).then_inc(normalised, 1)

            def copy_hT(t, par, first):
                dve.wait_ge(h_turned, t + 1)
                if not first:
                    dve.wait_ge(z_done, t - 1)
                dve.tensor_copy(hT[:, par, :, :], hT_ps[:, :, :]).then_inc(hT_copied, 1)

            def finish(t, tt, par, first):
                dve.wait_ge(rstd_ready, t + 1)
                if not first:
                    dve.wait_ge(out_stored[par], 16 * tt)
                dve.tensor_scalar(fin[:, par, :], y[:, par, :], mv[:, par, 0:1], rstd[:, par:par + 1],
                                  ALU.subtract, ALU.mult).then_inc(fin_ready, 1)

            def tile(t, tt, par, first, very_first, left):
                if left >= 1:
                    copy_hT(t + 1, 1 - par, very_first)
                if left >= 2:
                    normalise(t + 2, tt + 1, par, False)
                dve.wait_ge(z_done, t + 1)
                dve.tensor_tensor(z[:, par, :].rearrange("p (c f) -> p c f", c=CH), z_ps[:, par, :, :],
                                  bias[:, :].rearrange("p (c f) -> p c f", c=CH), ALU.add).then_inc(z_ready, 1)
                dve.wait_ge(z_ready, t + 1)
                dve.tensor_scalar(neg[:, par, :], z[:, par, :], 0.0, None, ALU.min).then_inc(neg_ready, 1)
                dve.wait_ge(x_in[par], 16 * (tt + 1))
                dve.scalar_tensor_tensor(pos[:, par, :], z[:, par, :], 0.0, xin[:, par, :],
                                         ALU.max, ALU.add).then_inc(pos_ready, 1)
                if not very_first:
                    finish(t - 1, tt if par else tt - 1, 1 - par, first)
                dve.wait_ge(exp_ready, t + 1)
                dve.wait_ge(pos_ready, t + 1)
                dve.scalar_tensor_tensor(y[:, par, :], e[:, par, :], -1.0, pos[:, par, :],
                                         ALU.add, ALU.add).then_inc(y_ready, 1)
                dve.wait_ge(y_ready, t + 1)
                for c in range(CH):
                    dve.bn_stats(stats[:, par, c, :], y[:, par, c * 512:(c + 1) * 512]).then_inc(stats_ready, 1)
                dve.drain()
                dve.bn_aggr(mv[:, par, :], stats[:, par, :, :]).then_inc(mv_ready, 1)
                dve.wait_ge(mv_ready, t + 1)
                dve.tensor_scalar(var[:, par:par + 1], mv[:, par, 1:2], EPS, None, ALU.add).then_inc(var_ready, 1)

            normalise(0, 0, 0, True)
            normalise(1, 0, 1, True)
            dve.wait_ge(b_in, 16)
            copy_hT(0, 0, True)
            tile(0, 0, 0, True, True, 2)
            tile(1, 0, 1, True, False, 2)
            tile(2, 1, 0, True, False, 2)
            tile(3, 1, 1, False, False, 2)
            with dve.Fori(2, NT // 2 - 1) as tt:
                tile(2 * tt, tt, 0, False, False, 2)
                tile(2 * tt + 1, tt, 1, False, False, 2)
            tile(NT - 2, NT // 2 - 1, 0, False, False, 1)
            tile(NT - 1, NT // 2 - 1, 1, False, False, 0)
            finish(NT - 1, NT // 2 - 1, 1, False)

        @block.scalar
        def _(act):
            def tile(t, par, first):
                act.wait_ge(neg_ready, t + 1)
                if not first:
                    act.wait_ge(y_ready, t - 1)
                act.activation(e[:, par, :], neg[:, par, :], ACT.Exp).then_inc(exp_ready, 1)

            tile(0, 0, True)
            tile(1, 1, True)
            with act.Fori(1, NT // 2) as tt:
                tile(2 * tt, 0, False)
                tile(2 * tt + 1, 1, False)

        @block.gpsimd
        def _(pool):
            pool.memset(half[:, 0:1], -0.5).then_inc(const_made, 1)
            pool.wait_ge(const_made, 1)

            def gather(t, par, first):
                if not first:
                    pool.wait_ge(pos_ready, t - 1)
                pool.tensor_copy(own_t[:, par:par + 1], own[:, bass.ds(t, 1), 0]).then_inc(own_ready, 1)
                pool.wait_ge(own_ready, t + 1)
                pool.sem_inc(carried, 1)
                pool.indirect_dma_start(xin[:, par, :], None, x,
                                        bass.IndirectOffsetOnAxis(ap=own_t[:, par:par + 1], axis=0),
                                        bounds_check=N - 1).then_inc(x_in[par], 16)

            def root(t, par, first):
                pool.wait_ge(var_ready, t + 1)
                if not first:
                    pool.wait_ge(fin_ready, t - 1)
                pool.tensor_tensor(rstd[:, par:par + 1], var[:, par:par + 1], half[:, 0:1], ALU.pow).then_inc(rstd_ready, 1)

            def scatter(t, tt, par, first):
                if not first:
                    pool.wait_ge(out_stored[par], 16 * tt)
                pool.tensor_copy(own_s[:, par:par + 1], own[:, bass.ds(t, 1), 0]).then_inc(own_s_ready, 1)
                pool.wait_ge(fin_ready, t + 1)
                pool.wait_ge(own_s_ready, t + 1)
                pool.sem_inc(carried, 1)
                pool.indirect_dma_start(out, bass.IndirectOffsetOnAxis(ap=own_s[:, par:par + 1], axis=0),
                                        fin[:, par, :], None, bounds_check=N - 1).then_inc(out_stored[par], 16)

            pool.wait_ge(own_in, 16)
            gather(0, 0, True)
            gather(1, 1, True)
            gather(2, 0, False)
            root(0, 0, True)
            gather(3, 1, False)
            root(1, 1, True)
            scatter(0, 0, 0, True)
            gather(4, 0, False)
            root(2, 0, False)
            scatter(1, 0, 1, True)
            gather(5, 1, False)
            root(3, 1, False)
            scatter(2, 1, 0, False)
            with pool.Fori(2, NT // 2 - 1) as tt:
                gather(2 * tt + 2, 0, False)
                root(2 * tt, 0, False)
                scatter(2 * tt - 1, tt - 1, 1, False)
                gather(2 * tt + 3, 1, False)
                root(2 * tt + 1, 1, False)
                scatter(2 * tt, tt, 0, False)
            root(NT - 2, 0, False)
            scatter(NT - 3, NT // 2 - 2, 1, False)
            root(NT - 1, 1, False)
            scatter(NT - 2, NT // 2 - 1, 0, False)
            scatter(NT - 1, NT // 2 - 1, 1, False)
            pool.wait_ge(out_stored[0], 16 * (NT // 2))
            pool.wait_ge(out_stored[1], 16 * (NT // 2))


_INS = ["x", "adj", "L0_gnn_W_seq", "L0_gnn_a1", "L0_gnn_a2", "L0_gnn_W_out", "L0_gnn_b_out"]


def kernel(**inputs):
    import numpy as np
    import concourse.bacc as bacc
    from concourse.bass_utils import run_bass_kernel_spmd

    nc = bacc.Bacc("TRN2", target_bir_lowering=False, num_devices=1)
    arrays, args = {}, []
    for name in _INS:
        a = np.ascontiguousarray(inputs[name])
        arrays[f"in_{name}_dram"] = a
        args.append(nc.dram_tensor(f"in_{name}_dram", a.shape, mybir.dt.from_np(a.dtype), kind="ExternalInput").ap())
    shape = inputs["x"].shape
    args.append(nc.dram_tensor("out_0_dram", shape, F32, kind="ExternalOutput").ap())
    gat_layer(nc, *args)
    r = run_bass_kernel_spmd(nc, [arrays], core_ids=[0])
    return r.results[0]["out_0_dram"]
```

```python
from contextlib import ExitStack

import concourse.bass as bass
from concourse import mybir

ALU = mybir.AluOpType
ACT = mybir.ActivationFunctionType
AX = mybir.AxisListType
F32 = mybir.dt.float32
BF16 = mybir.dt.bfloat16
F16 = mybir.dt.float16
U32 = mybir.dt.uint32
I32 = mybir.dt.int32

P = 128
HEADS = 16
ALPHA = 0.2
EPS = 1e-5
QUARTERS = 4
SLOTS = 24
HARD = SLOTS + 1
GROUP = 4
REST = 2
UNIT = 16
W_LIFT = 1024.0
H_LIFT = 64.0
NOWHERE = 1.0e6

R_IDX, R_VALID, R_A, R_C, R_SELF, R_LONE, R_ALL = 0, SLOTS, 2 * SLOTS, 2 * SLOTS + HEADS, 2 * SLOTS + 2 * HEADS, 2 * SLOTS + 2 * HEADS + 1, 96


def gat_layer(nc, x, adj, w_seq, a1, a2, w_out, b_out, out):
    N, D = x.shape
    NT = N // P
    KT = D // P
    SEQ = D + 2 * HEADS
    ROW = D + HEADS

    seq_d = nc.dram_tensor("seq_scratch", (N, SEQ), F32).ap()
    rec_d = nc.dram_tensor("record_scratch", (N, R_ALL), F32).ap()
    hid_d = nc.dram_tensor("hidden_scratch", (N, ROW), F32).ap()

    outer = ExitStack()
    with outer:
        def keep(name, shape, dt):
            return outer.enter_context(nc.sbuf_tensor(name, shape, dt))

        identf = keep("identf", [P, P], F32)
        identb = keep("identb", [P, P], BF16)
        ones = keep("ones", [P, P], F32)
        slots = keep("slots", [P, NT, SLOTS], F32)
        degree = keep("degree", [P, NT], F32)
        powers = keep("powers", [P, NT, 2, HEADS], F32)
        ctrl = keep("ctrl", [1, 4 * NT + 2], I32)

        project_and_search(nc, x, adj, w_seq, a1, a2, seq_d, identf, identb, ones, slots, degree, N, D, NT, KT, SEQ)
        w_hi = keep("w_out_hi", [P, KT, D], F16)
        w_lo = keep("w_out_lo", [P, KT, D], F16)
        with nc.sbuf_tensor("near", [P, 2, GROUP + REST, SEQ], F32) as near:
            sort_rows(nc, seq_d, rec_d, w_out, w_hi, w_lo, identf, ones, slots, degree, powers, ctrl, near,
                      N, D, NT, KT, SEQ)
            easy_rows(nc, seq_d, rec_d, hid_d, identf, identb, ctrl, near, N, D, NT, SEQ, ROW)
        hard_rows(nc, adj, seq_d, rec_d, hid_d, identf, ones, powers, ctrl, N, D, NT, ROW)
        output_layer(nc, x, w_hi, w_lo, b_out, rec_d, hid_d, out, identf, N, D, NT, KT, ROW)


def project_and_search(nc, x, adj, w_seq, a1, a2, seq_d, identf, identb, ones, slots, degree, N, D, NT, KT, SEQ):
    DH = D // HEADS
    SC = SEQ // 3
    QN = N // QUARTERS
    with ExitStack() as ctx:
        def sb(name, shape, dt):
            return ctx.enter_context(nc.sbuf_tensor(name, shape, dt))

        def ps(name, shape, dt):
            return ctx.enter_context(nc.psum_tensor(name, shape, dt))

        def sem(name):
            return ctx.enter_context(nc.semaphore(name))

        w = sb("w", [P, KT, SEQ], F32)
        avec = sb("avec", [P, 2, DH], F32)
        wa_tmp = sb("wa_tmp", [P, 2, HEADS, DH], F32)
        xin = sb("xin", [P, 2, D], F32)
        w_hi = sb("w_hi", [P, KT, SEQ], F16)
        w_lo = sb("w_lo", [P, KT, SEQ], F16)
        xT_hi = sb("xT_hi", [P, 2, KT, P], F16)
        xT_lo = sb("xT_lo", [P, 2, KT, P], F16)
        adj_in = sb("adj_in", [P, 2, N], F32)
        number = sb("number", [P, N], F32)
        numbered = sb("numbered", [P, 2, N], F32)
        unused = sb("unused", [P, N], BF16)
        row_sum = sb("row_sum", [P, 2], F32)
        cand = sb("cand", [P, 3, 8 * QUARTERS], F32)
        found = sb("found", [P, SLOTS], F32)
        seq = sb("seq", [P, 2, SEQ], F32)
        xT_ps = ps("xT_ps", [P, 2, KT // 2, P], F32)
        seq_ps = ps("seq_ps", [P, 2, 3, 512], F32)

        ident_made = sem("ident_made")
        number_made = sem("number_made")
        w_in = [sem(f"w_in{k}") for k in range(KT)]
        a_in = sem("a_in")
        a2_mul = sem("a2_mul")
        a1_mul = sem("a1_mul")
        wa_sum = sem("wa_sum")
        w_high = sem("w_high")
        w_split = sem("w_split")
        x_in = [sem("x_in0"), sem("x_in1")]
        adj_arrived = [sem("adj_in0"), sem("adj_in1")]
        x_turned = sem("x_turned")
        xT_high = sem("xT_high")
        xT_copied = sem("xT_copied")
        summed = sem("summed")
        is_numbered = sem("is_numbered")
        passed = sem("passed")
        searched = sem("searched")
        kept = sem("kept")
        seq_done = sem("seq_done")
        seq_copied = sem("seq_copied")
        seq_out = [sem("seq_out0"), sem("seq_out1")]

        block = ctx.enter_context(nc.Block())

        @block.gpsimd
        def _(pool):
            pool.memset(identf[:, :], 0.0).then_inc(ident_made, 1)
            pool.memset(identb[:, :], 0.0).then_inc(ident_made, 1)
            pool.memset(ones[:, :], 1.0).then_inc(ident_made, 1)
            pool.wait_ge(ident_made, 3)
            for m in (identf, identb):
                pool.affine_select(out=m[:, :], in_=m[:, :], compare_op=ALU.not_equal, fill=1.0,
                                   base=0, pattern=[[-1, P]], channel_multiplier=1).then_inc(ident_made, 1)
            pool.wait_ge(a_in, 32)
            for k in range(KT):
                if k == 1:
                    pool.iota(numbered[:, 0, :].bitcast(I32), pattern=[[1, N]], base=1, channel_multiplier=0
                              ).then_inc(number_made, 1)
                pool.wait_ge(w_in[k], 16)
                if k:
                    pool.wait_ge(wa_sum, 2 * k)
                pool.tensor_tensor(wa_tmp[:, 1, :, :], w[:, k, 0:D].rearrange("p (h d) -> p h d", h=HEADS),
                                   avec[:, 1:2, :].broadcast_to([P, HEADS, DH]), ALU.mult).then_inc(a1_mul, 1)
            pool.wait_ge(number_made, 2)

            def enumerate_columns(t, tt, par, first):
                pool.wait_ge(adj_arrived[par], 16 * (tt + 1))
                if not first:
                    pool.wait_ge(searched, t - 1)
                pool.tensor_tensor(numbered[:, par, :], adj_in[:, par, :], number[:, :], ALU.mult).then_inc(is_numbered, 1)

            enumerate_columns(0, 0, 0, True)
            enumerate_columns(1, 0, 1, True)
            with pool.Fori(1, NT // 2) as tt:
                enumerate_columns(2 * tt, tt, 0, False)
                enumerate_columns(2 * tt + 1, tt, 1, False)

        @block.sync
        def _(sp):
            sp.dma_start(avec[:, 0, :], a2.partition_broadcast(P)).then_inc(a_in, 16)
            sp.dma_start(avec[:, 1, :], a1.partition_broadcast(P)).then_inc(a_in, 16)

            def loads(t, par, first):
                if not first:
                    sp.wait_ge(x_turned, t - 1)
                sp.dma_start(xin[:, par, :], x[bass.ds(t * P, P), :]).then_inc(x_in[par], 16)
                if not first:
                    sp.wait_ge(is_numbered, t - 1)
                    sp.wait_ge(summed, t - 1)
                sp.dma_start(adj_in[:, par, :], adj[bass.ds(t * P, P), :]).then_inc(adj_arrived[par], 16)

            for k in range(KT):
                sp.dma_start(w[:, k, 0:D], w_seq[k * P:(k + 1) * P, :]).then_inc(w_in[k], 16)
                if k == 0:
                    sp.dma_start(xin[:, 0, :], x[0:P, :]).then_inc(x_in[0], 16)
            sp.dma_start(adj_in[:, 0, :], adj[0:P, :]).then_inc(adj_arrived[0], 16)
            loads(1, 1, True)
            with sp.Fori(1, NT // 2) as tt:
                loads(2 * tt, 0, False)
                loads(2 * tt + 1, 1, False)

        @block.tensor
        def _(pe):
            pe.wait_ge(ident_made, 5)

            def turn(t, tt, par, very_first):
                pe.wait_ge(x_in[par], 16 * (tt + 1))
                if not very_first:
                    pe.wait_ge(xT_copied, t)
                for k in range(KT):
                    mm = pe.transpose(xT_ps[:, k // (KT // 2), k % (KT // 2), :], xin[:, par, k * P:(k + 1) * P],
                                      identf[:, :])
                mm.then_inc(x_turned, 1)

            def project(t, par, first, very_first=False):
                if not first:
                    pe.wait_ge(seq_copied, t - 1)
                pe.wait_ge(xT_copied, t + 1)
                for k in range(KT):
                    if very_first:
                        pe.wait_ge(w_split, k + 1)
                    for c in range(3):
                        for part in (w_hi, w_lo):
                            pe.matmul(seq_ps[:, par, c, 0:SC], xT_hi[:, par, k, :], part[:, k, c * SC:(c + 1) * SC],
                                      start=(k == 0 and part is w_hi), stop=False)
                    for c in range(3):
                        mm = pe.matmul(seq_ps[:, par, c, 0:SC], xT_lo[:, par, k, :], w_hi[:, k, c * SC:(c + 1) * SC],
                                       start=False, stop=(k == KT - 1))
                mm.then_inc(seq_done, 1)

            turn(0, 0, 0, True)
            turn(1, 0, 1, False)
            project(0, 0, True, very_first=True)
            turn(2, 1, 0, False)
            project(1, 1, True)
            turn(3, 1, 1, False)
            project(2, 0, False)
            with pe.Fori(2, NT // 2) as tt:
                turn(2 * tt, tt, 0, False)
                project(2 * tt - 1, 1, False)
                turn(2 * tt + 1, tt, 1, False)
                project(2 * tt, 0, False)
            project(NT - 1, 1, False)

        @block.vector
        def _(dve):
            def weights(k):
                dve.wait_ge(w_in[k], 16)
                if k:
                    dve.wait_ge(wa_sum, 2 * k)
                dve.tensor_tensor(wa_tmp[:, 0, :, :], w[:, k, 0:D].rearrange("p (h d) -> p h d", h=HEADS),
                                  avec[:, 0:1, :].broadcast_to([P, HEADS, DH]), ALU.mult).then_inc(a2_mul, 1)
                dve.wait_ge(a1_mul, k + 1)
                dve.wait_ge(a2_mul, k + 1)
                for s in range(2):
                    dve.tensor_reduce(w[:, k, D + s * HEADS:D + (s + 1) * HEADS], wa_tmp[:, s, :, :],
                                      AX.X, ALU.add).then_inc(wa_sum, 1)
                dve.wait_ge(w_high, k + 1)
                dve.scalar_tensor_tensor(w_lo[:, k, :], w[:, k, :], W_LIFT, w_hi[:, k, :],
                                         ALU.mult, ALU.subtract).then_inc(w_split, 1)

            def copy_xT(t, par, first):
                if not first:
                    dve.wait_ge(seq_done, t - 1)
                dve.wait_ge(xT_high, t + 1)
                dve.tensor_tensor(xT_lo[:, par, :, :].rearrange("p (b k) i -> p b k i", b=2), xT_ps[:, :, :, :],
                                  xT_hi[:, par, :, :].rearrange("p (b k) i -> p b k i", b=2),
                                  ALU.subtract).then_inc(xT_copied, 1)

            def search(t, tt, par):
                dve.wait_ge(is_numbered, t + 1)
                dve.sem_inc(passed, 1)
                for q in range(QUARTERS):
                    mx = dve.max(cand[:, 0, 8 * q:8 * (q + 1)], numbered[:, par, q * QN:(q + 1) * QN])
                mx.then_inc(searched, 1)
                dve.drain()
                for r in range(SLOTS // 8):
                    dve.max(found[:, 8 * r:8 * (r + 1)], cand[:, r, :])
                    dve.drain()
                    if r < SLOTS // 8 - 1:
                        dve.match_replace(cand[:, r + 1, :], found[:, 8 * r:8 * (r + 1)], cand[:, r, :], 0.0)
                        dve.drain()
                dve.tensor_copy(slots[:, bass.ds(t, 1), :], found[:, :].rearrange("p (o s) -> p o s", o=1))
                dve.wait_ge(summed, t + 1)
                dve.tensor_copy(degree[:, bass.ds(t, 1)], row_sum[:, par:par + 1]).then_inc(kept, 1)
                dve.drain()

            dve.wait_ge(a_in, 32)
            weights(0)
            copy_xT(0, 0, True)
            for k in range(1, KT):
                weights(k)
            copy_xT(1, 1, True)
            search(0, 0, 0)
            copy_xT(2, 0, False)
            search(1, 0, 1)
            with dve.Fori(1, NT // 2 - 1) as tt:
                copy_xT(2 * tt + 1, 1, False)
                search(2 * tt, tt, 0)
                copy_xT(2 * tt + 2, 0, False)
                search(2 * tt + 1, tt, 1)
            copy_xT(NT - 1, 1, False)
            search(NT - 2, NT // 2 - 1, 0)
            search(NT - 1, NT // 2 - 1, 1)

        @block.scalar
        def _(act):
            def add_up(t, tt, par, first, very_first):
                act.wait_ge(adj_arrived[par], 16 * (tt + 1))
                if not first:
                    act.wait_ge(kept, t - 1)
                if not very_first:
                    act.wait_ge(summed, t)
                act.activation(unused[:, :], adj_in[:, par, :], ACT.Copy,
                               accum_out=row_sum[:, par:par + 1]).then_inc(summed, 1)

            def high(t, par, first):
                act.wait_ge(x_turned, t + 1)
                if not first:
                    act.wait_ge(seq_done, t - 1)
                act.copy(xT_hi[:, par, :, :].rearrange("p (b k) i -> p b k i", b=2), xT_ps[:, :, :, :]).then_inc(xT_high, 1)

            def evacuate(t, tt, par, first):
                act.wait_ge(seq_done, t + 1)
                if not first:
                    act.wait_ge(seq_out[par], 16 * tt)
                act.activation(seq[:, par, :].rearrange("p (c s) -> p c s", c=3), seq_ps[:, par, :, 0:SC], ACT.Copy,
                               scale=1.0 / W_LIFT).then_inc(seq_copied, 1)
                act.wait_ge(seq_copied, t + 1)
                act.dma_start(seq_d[bass.ds(t * P, P), :], seq[:, par, :]).then_inc(seq_out[par], 16)

            for k in range(KT):
                act.wait_ge(wa_sum, 2 * (k + 1))
                act.activation(w_hi[:, k, :], w[:, k, :], ACT.Copy, scale=W_LIFT).then_inc(w_high, 1)
                if k == 0:
                    high(0, 0, True)
                if k == 3:
                    act.wait_ge(number_made, 1)
                    act.copy(number[:, :], numbered[:, 0, :].bitcast(I32)).then_inc(number_made, 1)
            high(1, 1, True)
            add_up(0, 0, 0, True, True)
            add_up(1, 0, 1, True, False)
            evacuate(0, 0, 0, True)
            high(2, 0, False)
            add_up(2, 1, 0, False, False)
            evacuate(1, 0, 1, True)
            high(3, 1, False)
            add_up(3, 1, 1, False, False)
            evacuate(2, 1, 0, False)
            with act.Fori(2, NT // 2) as tt:
                high(2 * tt, 0, False)
                add_up(2 * tt, tt, 0, False, False)
                evacuate(2 * tt - 1, tt - 1, 1, False)
                high(2 * tt + 1, 1, False)
                add_up(2 * tt + 1, tt, 1, False, False)
                evacuate(2 * tt, tt, 0, False)
            evacuate(NT - 1, NT // 2 - 1, 1, False)
            for par in range(2):
                act.wait_ge(seq_out[par], 16 * (NT // 2))


def sort_rows(nc, seq_d, rec_d, w_out, w_hi, w_lo, identf, ones, slots, degree, powers, ctrl, near,
              N, D, NT, KT, SEQ):
    KEYS = HARD
    KC = KEYS * NT
    HC = KC // 2
    UNITS = N // UNIT
    with ExitStack() as ctx:
        def sb(name, shape, dt):
            return ctx.enter_context(nc.sbuf_tensor(name, shape, dt))

        def ps(name, shape, dt):
            return ctx.enter_context(nc.psum_tensor(name, shape, dt))

        def sem(name):
            return ctx.enter_context(nc.semaphore(name))

        scores = sb("scores", [P, NT, 2, HEADS], F32)
        w = sb("w_out_sb", [P, KT, D], F32)
        part_max = sb("part_max", [P, HEADS], F32)
        head_max = sb("head_max", [HEADS, 1], F32)
        diag_max = sb("diag_max", [HEADS, HEADS], F32)
        max_s2 = sb("max_s2", [P, HEADS], F32)
        shifted = sb("shifted", [P, NT, HEADS], F32)
        bound = sb("bound", [P, NT, HEADS], F32)
        expo = sb("expo", [P, NT, 2, HEADS], F32)
        record = sb("record", [P, NT, R_ALL], F32)
        self_i = sb("self_i", [P, NT], I32)
        keys_i = sb("keys_i", [P, KEYS], I32)
        keys = sb("keys", [P, KEYS], F32)
        last_i = sb("last_i", [1, NT], I32)
        last = sb("last", [1, NT], F32)
        units_i = sb("units_i", [1, UNITS], I32)
        units = sb("units", [1, UNITS], F32)
        before = sb("before", [P, P], BF16)
        all_b = sb("all_b", [P, P], BF16)
        empty = sb("empty", [P, NT, SLOTS], F32)
        captured = sb("captured", [P, NT], F32)
        complete = sb("complete", [P, NT], F32)
        easy = sb("easy", [P, NT], F32)
        key = sb("key", [P, NT], F32)
        hot = sb("hot", [P, KEYS, NT], BF16)
        scan = sb("scan", [P, 2, KC], F32)
        total = sb("total", [P, KC], F32)
        place = sb("place", [P, KEYS, NT], F32)
        rank = sb("rank", [P, NT], F32)
        rank_u = sb("rank_u", [P, NT], U32)
        clipped = sb("clipped", [1, NT], F32)
        needed = sb("needed", [1, 2, 2, NT], F32)
        extent = sb("extent", [1, 4, NT], F32)
        before_t = sb("before_t", [1, 2, 2, NT], F32)
        n_hard = sb("n_hard", [1, 1], F32)
        unit_on = sb("unit_on", [1, UNITS], F32)
        n_units = sb("n_units", [1, 1], F32)
        small_ps = ps("small_ps", [P, P], F32)
        max_ps = ps("max_ps", [P, HEADS], F32)
        pre_ps = ps("pre_ps", [P, 2, 512], F32)
        tot_ps = ps("tot_ps", [P, 2, 512], F32)

        scores_in = sem("scores_in")
        consts = sem("consts")
        step = sem("step")
        max_turned = sem("max_turned")
        max_spread = sem("max_spread")
        counted = sem("counted")
        exp_done = sem("exp_done")
        powers_out = sem("powers_out")
        ranked = sem("ranked")
        scattered = sem("scattered")
        w_in = sem("w_out_in")
        w_high = sem("w_out_high")

        block = ctx.enter_context(nc.Block())
        seq_v = seq_d.rearrange("(t p) c -> p t c", p=P)
        marks = {}

        @block.gpsimd
        def _(pool):
            pool.iota(self_i[:, :], pattern=[[P, NT]], base=0, channel_multiplier=1).then_inc(consts, 1)
            pool.iota(keys_i[:, :], pattern=[[1, KEYS]], base=1, channel_multiplier=0).then_inc(consts, 1)
            pool.iota(last_i[:, :], pattern=[[P, NT]], base=P - 1, channel_multiplier=0).then_inc(consts, 1)
            pool.iota(units_i[:, :], pattern=[[UNIT, UNITS]], base=0, channel_multiplier=0).then_inc(consts, 1)
            pool.memset(all_b[:, :], 1.0).then_inc(consts, 1)
            pool.memset(record[:, :, R_LONE:R_ALL], 0.0).then_inc(consts, 1)
            pool.wait_ge(consts, 6)
            pool.affine_select(out=before[:, :], in_=all_b[:, :], compare_op=ALU.is_gt, fill=0.0,
                               base=0, pattern=[[1, P]], channel_multiplier=-1).then_inc(consts, 1)
            pool.wait_ge(ranked, 1)
            pool.wait_ge(exp_done, 3)
            for t in range(NT):
                pool.indirect_dma_start(rec_d, bass.IndirectOffsetOnAxis(ap=rank_u[:, t:t + 1], axis=0),
                                        record[:, t, :], None, bounds_check=N - 1).then_inc(scattered, 16)
            pool.wait_ge(scattered, 16 * NT)

        @block.sync
        def _(sp):
            sp.dma_start(scores[:, :, :, :].rearrange("p t s h -> p t (s h)"), seq_v[:, :, D:SEQ]).then_inc(scores_in, 16)
            sp.dma_start(w[:, :, :], w_out.rearrange("(k p) d -> p k d", p=P)).then_inc(w_in, 16)
            sp.wait_ge(exp_done, 2)
            sp.dma_start(seq_v[:, :, D:SEQ], powers[:, :, :, :].rearrange("p t s h -> p t (s h)")).then_inc(powers_out, 16)
            sp.wait_ge(powers_out, 16)

        @block.vector
        def _(dve):
            n = 0

            def done(ins, name=None):
                nonlocal n
                ins.then_inc(step, 1)
                n += 1
                if name:
                    marks[name] = n

            s2 = scores[:, :, 0, :]
            s1 = scores[:, :, 1, :]
            dve.wait_ge(consts, 7)
            done(dve.tensor_scalar(record[:, :, R_VALID:R_A], slots[:, :, :], 0.0, None, ALU.is_gt))
            done(dve.tensor_scalar(empty[:, :, :], slots[:, :, :], 0.0, NOWHERE, ALU.is_equal, ALU.mult))
            done(dve.tensor_copy(keys[:, :], keys_i[:, :]))
            done(dve.tensor_copy(last[:, :], last_i[:, :]))
            done(dve.tensor_copy(units[:, :], units_i[:, :]))
            dve.wait_ge(step, n)
            done(dve.tensor_reduce(captured[:, :], record[:, :, R_VALID:R_A], AX.X, ALU.add))
            done(dve.scalar_tensor_tensor(record[:, :, R_IDX:R_VALID].bitcast(U32), slots[:, :, :], -1.0,
                                          empty[:, :, :], ALU.add, ALU.add))
            dve.wait_ge(step, n)
            done(dve.tensor_tensor(complete[:, :], captured[:, :], degree[:, :], ALU.is_equal))
            dve.wait_ge(step, n)
            done(dve.scalar_tensor_tensor(easy[:, :], degree[:, :], 0.0, complete[:, :], ALU.is_gt, ALU.mult))
            dve.wait_ge(step, n)
            done(dve.scalar_tensor_tensor(key[:, :], degree[:, :], -float(HARD), easy[:, :], ALU.add, ALU.mult))
            dve.wait_ge(step, n)
            done(dve.tensor_scalar(keys[:, :], keys[:, :], -float(HARD), None, ALU.add))
            dve.wait_ge(step, n)
            done(dve.tensor_tensor(hot[:, :, :], key[:, None, :].broadcast_to([P, KEYS, NT]),
                                   keys[:, :, None].broadcast_to([P, KEYS, NT]), ALU.is_equal), "hot")
            done(dve.tensor_copy(record[:, :, R_SELF].bitcast(U32), self_i[:, :]))
            done(dve.tensor_scalar(record[:, :, R_LONE], degree[:, :], 0.0, None, ALU.is_equal))
            dve.wait_ge(scores_in, 16)
            done(dve.tensor_reduce(part_max[:, :], s2.rearrange("p t h -> p h t"), AX.X, ALU.max), "part_max")
            dve.wait_ge(max_turned, 1)
            done(dve.tensor_reduce(head_max[:, :], small_ps[0:HEADS, :], AX.X, ALU.max))
            dve.wait_ge(step, n)
            done(dve.tensor_scalar(diag_max[:, :], identf[0:HEADS, 0:HEADS], head_max[:, 0:1], None, ALU.mult), "diag_max")
            dve.wait_ge(max_spread, 1)
            done(dve.tensor_copy(max_s2[:, :], max_ps[:, :]))
            dve.wait_ge(step, n)
            m = max_s2[:, None, :].broadcast_to([P, NT, HEADS])
            done(dve.tensor_tensor(shifted[:, :, :], s2, m, ALU.subtract), "shifted")
            done(dve.tensor_tensor(bound[:, :, :], s1, m, ALU.add))
            dve.wait_ge(step, n)
            done(dve.tensor_scalar(expo[:, :, 0, :], bound[:, :, :], 0.0, 1.0 - ALPHA, ALU.min, ALU.mult))
            done(dve.tensor_scalar(expo[:, :, 1, :], bound[:, :, :], 0.0, ALPHA - 1.0, ALU.max, ALU.mult), "expo")
            dve.wait_ge(counted, 1)
            done(dve.tensor_copy(total[:, :].rearrange("p (b c) -> p b c", b=2), tot_ps[:, :, 0:HC]))
            dve.wait_ge(step, n)
            done(dve.tensor_copy(scan[:, 0, :], total[:, :]))
            cur, d = 0, 1
            while d < KC:
                dve.wait_ge(step, n)
                done(dve.tensor_tensor(scan[:, 1 - cur, d:KC], scan[:, cur, d:KC], scan[:, cur, 0:KC - d], ALU.add))
                done(dve.tensor_copy(scan[:, 1 - cur, 0:d], scan[:, cur, 0:d]))
                cur, d = 1 - cur, 2 * d
            dve.wait_ge(step, n)
            done(dve.tensor_tensor(scan[:, 1 - cur, :], scan[:, cur, :], total[:, :], ALU.subtract))
            first = scan[:, 1 - cur, :]
            dve.wait_ge(step, n)
            done(dve.tensor_tensor(total[:, :].rearrange("p (b c) -> p b c", b=2), pre_ps[:, :, 0:HC],
                                   first.rearrange("p (b c) -> p b c", b=2), ALU.add))
            dve.wait_ge(step, n)
            done(dve.tensor_tensor(place[:, :, :], total[:, :].rearrange("p (k t) -> p k t", k=KEYS), hot[:, :, :], ALU.mult))
            dve.wait_ge(step, n)
            done(dve.tensor_reduce(rank[:, :], place[:, :, :].rearrange("p k t -> p t k"), AX.X, ALU.add))
            dve.wait_ge(step, n)
            dve.tensor_copy(rank_u[:, :], rank[:, :]).then_inc(ranked, 1)
            row0 = scan[0:1, 1 - cur, :]
            hard0 = row0[:, (HARD - 1) * NT:(HARD - 1) * NT + 1]
            done(dve.tensor_scalar(n_hard[:, :], hard0, -1.0, float(N), ALU.mult, ALU.add))
            done(dve.tensor_scalar(clipped[:, :], hard0.broadcast_to([1, NT]), -1.0, None, ALU.add))
            dve.wait_ge(step, n)
            done(dve.tensor_tensor(clipped[:, :], clipped[:, :], last[:, :], ALU.min))
            done(dve.memset(needed[:, 0, :, :], 0.0))
            for j in range(SLOTS // GROUP):
                dve.wait_ge(step, n)
                for w2 in range(2):
                    k = j * GROUP + w2 * REST
                    done(dve.scalar_tensor_tensor(needed[:, (j + 1) % 2, w2, :], clipped[:, :], row0[:, k * NT:k * NT + 1],
                                                  needed[:, j % 2, w2, :], ALU.is_ge, ALU.add))
            pairs = needed[:, (SLOTS // GROUP) % 2, :, :]
            dve.wait_ge(step, n)
            done(dve.tensor_scalar(extent[:, 0, :], pairs[:, 1, :], 1.0, None, ALU.max))
            dve.wait_ge(step, n)
            done(dve.tensor_tensor(extent[:, 2, :], pairs[:, 0, :], extent[:, 0, :], ALU.subtract))
            dve.wait_ge(step, n)
            done(dve.tensor_scalar(extent[:, 1, :], extent[:, 2, :], 0.0, None, ALU.max))
            dve.wait_ge(step, n)
            done(dve.tensor_copy(before_t[:, 0, 0, :], extent[:, 1, :]))
            done(dve.tensor_copy(before_t[:, 0, 1, :], extent[:, 0, :]))
            dve.wait_ge(step, n)
            done(dve.tensor_scalar(extent[:, 2:4, :], before_t[:, 0, :, :], -1.0, None, ALU.mult))
            cur, d = 0, 2
            while d < NT:
                dve.wait_ge(step, n)
                done(dve.tensor_tensor(before_t[:, 1 - cur, :, d:NT], before_t[:, cur, :, d:NT], before_t[:, cur, :, 0:NT - d], ALU.add))
                done(dve.tensor_copy(before_t[:, 1 - cur, :, 0:d], before_t[:, cur, :, 0:d]))
                cur, d = 1 - cur, 2 * d
            dve.wait_ge(step, n)
            per_tile = ctrl[:, 0:4 * NT].rearrange("o (t c) -> o c t", c=4)
            done(dve.tensor_copy(per_tile[:, 0:2, :], extent[:, 0:2, :]))
            done(dve.tensor_tensor(per_tile[:, 2:4, :], before_t[:, cur, :, :], extent[:, 2:4, :], ALU.add))
            done(dve.tensor_scalar(unit_on[:, :], units[:, :], n_hard[:, 0:1], None, ALU.is_lt))
            dve.wait_ge(step, n)
            done(dve.tensor_reduce(n_units[:, :], unit_on[:, :], AX.X, ALU.add))
            dve.wait_ge(step, n)
            done(dve.tensor_scalar(ctrl[:, 4 * NT:4 * NT + 1], n_units[:, :], 1.0, None, ALU.max))
            done(dve.memset(near[:, :, :, :], 0.0))
            dve.wait_ge(w_in, 16)
            for k in range(KT):
                dve.wait_ge(w_high, k + 1)
                done(dve.scalar_tensor_tensor(w_lo[:, k, :], w[:, k, :], W_LIFT, w_hi[:, k, :], ALU.mult, ALU.subtract))

        @block.tensor
        def _(pe):
            pe.wait_ge(step, marks["hot"])
            for b in range(2):
                flat = hot[:, :, :].rearrange("p k t -> p (k t)")[:, b * HC:(b + 1) * HC]
                pe.matmul(pre_ps[:, b, 0:HC], before[:, :], flat, start=True, stop=True)
                mm = pe.matmul(tot_ps[:, b, 0:HC], all_b[:, :], flat, start=True, stop=True)
            mm.then_inc(counted, 1)
            pe.wait_ge(step, marks["part_max"])
            pe.transpose(small_ps[0:HEADS, :], part_max[:, :], identf[:, :]).then_inc(max_turned, 1)
            pe.wait_ge(step, marks["diag_max"])
            pe.matmul(max_ps[:, :], ones[0:HEADS, :], diag_max[:, :], start=True, stop=True).then_inc(max_spread, 1)

        @block.scalar
        def _(act):
            act.wait_ge(step, marks["shifted"])
            act.activation(powers[:, :, 0, :], shifted[:, :, :], ACT.Exp).then_inc(exp_done, 1)
            act.activation(powers[:, :, 1, :], shifted[:, :, :], ACT.Exp, scale=ALPHA).then_inc(exp_done, 1)
            act.wait_ge(step, marks["expo"])
            act.activation(record[:, :, R_A:R_SELF].rearrange("p t (s h) -> p t s h", s=2), expo[:, :, :, :],
                           ACT.Exp).then_inc(exp_done, 1)
            act.wait_ge(w_in, 16)
            for k in range(KT):
                act.activation(w_hi[:, k, :], w[:, k, :], ACT.Copy, scale=W_LIFT).then_inc(w_high, 1)


def easy_rows(nc, seq_d, rec_d, hid_d, identf, identb, ctrl, near, N, D, NT, SEQ, ROW):
    DH = D // HEADS
    MOST = SLOTS // GROUP
    BUFS = GROUP + REST
    DVE_HEADS = 3 * HEADS // 4
    DVE_D = DVE_HEADS * DH
    with ExitStack() as ctx:
        def sb(name, shape, dt):
            return ctx.enter_context(nc.sbuf_tensor(name, shape, dt))

        def sem(name):
            return ctx.enter_context(nc.semaphore(name))

        rec = sb("rec", [P, NT * R_ALL], F32)
        index = sb("index", [P, 2, BUFS], U32)
        both = sb("both", [P, 2, BUFS, 2, HEADS], F32)
        weight = sb("slot_weight", [P, 2, BUFS, HEADS], F32)
        prod = sb("prod", [P, 2, BUFS, D], F32)
        wsum = sb("wsum", [P, 2, HEADS], F32)
        wsum_all = sb("wsum_all", [P, NT, HEADS], F32)
        sumsT = sb("sumsT", [P, 2, D // P, P], F32)
        zero = sb("zero", [P, 512], BF16)
        sums = sb("sums", [P, 2, ROW], F32)
        accT = ctx.enter_context(nc.psum_tensor("accT", [P, 2, D // P, P], F32))
        back_ps = ctx.enter_context(nc.psum_tensor("back_ps", [P, 2, D // P, P], F32))

        def two(name):
            return [sem(f"{name}{par}") for par in range(2)]

        rec_in = [sem("rec_in0"), sem("rec_in1")]
        index_ready = two("index_ready")
        near_in = [[sem(f"near_in{par}_{s}") for s in range(BUFS)] for par in range(2)]
        near_done = two("near_done")
        act_done = two("act_done")
        both_ready = two("both_ready")
        weight_ready = two("weight_ready")
        wsum_ready = two("wsum_ready")
        wsum_final = sem("wsum_final")
        wsum_copied = sem("wsum_copied")
        prod_free = two("prod_free")
        zero_made = sem("zero_made")
        carried = sem("carried")
        acc_done = sem("acc_done")
        acc_copied = sem("acc_copied")
        turned_back = sem("turned_back")
        sums_copied = sem("sums_copied")
        sums_out = [sem("sums_out0"), sem("sums_out1")]

        block = ctx.enter_context(nc.Block())

        def extents(eng, tt):
            _, v = nc.values_load_multi_w_load_instructions(ctrl[0:1, bass.ds(8 * tt, 8)], engines=[eng.engine],
                                                            min_val=0, max_val=2 * MOST * NT)
            return [(nc.s_assert_within(v[4 * par], 1, MOST), v[4 * par + 1], v[4 * par + 2], v[4 * par + 3])
                    for par in range(2)]

        def slots_of(eng, extent, slot):
            count, rest, rests, groups = extent
            first = groups * GROUP + rests * REST
            with eng.Fori(0, count) as u:
                for s in range(GROUP):
                    n = first + u * GROUP + s
                    slot(s, n, u * GROUP + s, n + 1, groups + u + 1)
            with eng.If_ne(eng.to_reg(rest), 0):
                for s in range(GROUP, BUFS):
                    column = count * GROUP + (s - GROUP)
                    slot(s, first + column, column, first + GROUP, rests + 1)
            return first + count * GROUP + rest * REST

        def tiles(eng, tile):
            even, odd = extents(eng, 0)
            tile(0, 0, 0, True, even)
            tile(1, 0, 1, True, odd)
            with eng.Fori(1, NT // 2) as tt:
                even, odd = extents(eng, tt)
                tile(2 * tt, tt, 0, False, even)
                tile(2 * tt + 1, tt, 1, False, odd)

        @block.sync
        def _(sp):
            sp.dma_start(rec[:, 0:R_ALL], rec_d[0:P, :]).then_inc(rec_in[0], 16)
            sp.dma_start(rec[:, R_ALL:NT * R_ALL].rearrange("p (t r) -> p t r", r=R_ALL),
                         rec_d[P:N, :].rearrange("(t p) r -> p t r", p=P)).then_inc(rec_in[1], 16)

        @block.gpsimd
        def _(pool):
            def tile(t, tt, par, first, extent):
                if first:
                    pool.wait_ge(rec_in[par], 16)
                    pool.sem_inc(carried, 1)

                def slot(s, n, column, free, arrived):
                    pool.wait_ge(near_done[par], free)
                    pool.wait_ge(act_done[par], free)
                    pool.tensor_copy(index[:, par, s:s + 1], rec[:, bass.ds(t * R_ALL + column + R_IDX, 1)].bitcast(U32)
                                     ).then_inc(index_ready[par], 1)
                    pool.wait_ge(index_ready[par], n + 1)
                    pool.sem_inc(carried, 1)
                    pool.indirect_dma_start(near[:, par, s, :], None, seq_d,
                                            bass.IndirectOffsetOnAxis(ap=index[:, par, s:s + 1], axis=0),
                                            bounds_check=N - 1, oob_is_err=False).then_inc(near_in[par][s], 16)

                slots_of(pool, extent, slot)
            tiles(pool, tile)

        @block.vector
        def _(dve):
            dve.memset(zero[:, :], 0.0).then_inc(zero_made, 1)
            for par in range(2):
                dve.sem_inc(near_done[par], GROUP)
                dve.sem_inc(act_done[par], GROUP)
                dve.sem_inc(prod_free[par], GROUP)

            def tile(t, tt, par, first, extent):
                dve.memset(wsum[:, par, :], 0.0).then_inc(wsum_ready[par], 1)
                if first:
                    dve.wait_ge(rec_in[par], 16)
                    dve.sem_inc(carried, 1)

                def slot(s, n, column, free, arrived):
                    dve.wait_ge(near_in[par][s], arrived * 16)
                    dve.scalar_tensor_tensor(both[:, par, s, :, :].rearrange("p a h -> p (a h)"), near[:, par, s, D:SEQ],
                                             rec[:, bass.ds(t * R_ALL + column + R_VALID, 1)],
                                             rec[:, bass.ds(t * R_ALL + R_A, 2 * HEADS)], ALU.mult, ALU.mult
                                             ).then_inc(both_ready[par], 1)
                    dve.wait_ge(both_ready[par], n + 1)
                    dve.wait_ge(act_done[par], free)
                    dve.tensor_tensor(weight[:, par, s, :], both[:, par, s, 0, :], both[:, par, s, 1, :], ALU.max
                                      ).then_inc(weight_ready[par], 1)
                    dve.wait_ge(prod_free[par], free)
                    dve.wait_ge(weight_ready[par], n + 1)
                    dve.tensor_tensor(prod[:, par, s, 0:DVE_D].rearrange("p (h d) -> p h d", h=DVE_HEADS),
                                      near[:, par, s, 0:DVE_D].rearrange("p (h d) -> p h d", h=DVE_HEADS),
                                      weight[:, par, s, 0:DVE_HEADS].rearrange("p (h o) -> p h o", o=1
                                                                               ).broadcast_to([P, DVE_HEADS, DH]),
                                      ALU.mult).then_inc(near_done[par], 1)
                    dve.wait_ge(wsum_ready[par], n + 1 + tt)
                    dve.tensor_tensor(wsum[:, par, :], wsum[:, par, :], weight[:, par, s, :], ALU.add
                                      ).then_inc(wsum_ready[par], 1)

                so_far = slots_of(dve, extent, slot)
                dve.wait_ge(wsum_ready[par], so_far + tt + 1)
                dve.tensor_copy(wsum_all[:, bass.ds(t, 1), :], wsum[:, par:par + 1, :]).then_inc(wsum_final, 1)
            tiles(dve, tile)

        @block.tensor
        def _(pe):
            pe.wait_ge(zero_made, 1)

            def tile(t, tt, par, first, extent):
                if not first:
                    pe.wait_ge(acc_copied, t - 1)
                for c in range(2):
                    pe.matmul(accT[:, par, 4 * c:4 * (c + 1), :], identb[:, :], zero[:, :],
                              start=True, stop=False, skip_group_check=True)

                def slot(s, n, column, free, arrived):
                    pe.wait_ge(near_done[par], n + 1 + GROUP)
                    pe.wait_ge(act_done[par], n + 1 + GROUP)
                    for c in range(D // P):
                        mm = pe.matmul(accT[:, par, c, :], prod[:, par, s, c * P:(c + 1) * P], identf[:, :],
                                       start=False, stop=False, is_transpose=True, skip_group_check=True)
                    mm.then_inc(prod_free[par], 1)

                slots_of(pe, extent, slot)
                pe.matmul(accT[:, par, 0, 0:HEADS], identb[:, :], zero[:, 0:HEADS], start=False, stop=True,
                          skip_group_check=True).then_inc(acc_done, 1)

            def turn_back(t, par, first):
                pe.wait_ge(acc_copied, t + 1)
                if not first:
                    pe.wait_ge(sums_copied, t - 1)
                for c in range(D // P):
                    mm = pe.transpose(back_ps[:, par, c, :], sumsT[:, par, c, :], identf[:, :])
                mm.then_inc(turned_back, 1)

            even, odd = extents(pe, 0)
            tile(0, 0, 0, True, even)
            tile(1, 0, 1, True, odd)
            turn_back(0, 0, True)
            even, odd = extents(pe, 1)
            tile(2, 1, 0, False, even)
            turn_back(1, 1, True)
            tile(3, 1, 1, False, odd)
            turn_back(2, 0, False)
            with pe.Fori(2, NT // 2) as tt:
                even, odd = extents(pe, tt)
                tile(2 * tt, tt, 0, False, even)
                turn_back(2 * tt - 1, 1, False)
                tile(2 * tt + 1, tt, 1, False, odd)
                turn_back(2 * tt, 0, False)
            turn_back(NT - 1, 1, False)

        @block.scalar
        def _(act):
            def columns(t, par, first):
                act.wait_ge(acc_done, t + 1)
                if not first:
                    act.wait_ge(turned_back, t - 1)
                act.copy(sumsT[:, par, :, :], accT[:, par, :, :]).then_inc(acc_copied, 1)

            def rows(t, tt, par, first):
                if not first:
                    act.wait_ge(sums_out[par], 16 * tt)
                act.wait_ge(wsum_final, t + 1)
                act.copy(sums[:, par:par + 1, D:ROW], wsum_all[:, bass.ds(t, 1), :]).then_inc(wsum_copied, 1)
                act.wait_ge(turned_back, t + 1)
                act.copy(sums[:, par, 0:D], back_ps[:, par, :, :].rearrange("p c i -> p (c i)")).then_inc(sums_copied, 1)
                act.wait_ge(sums_copied, t + 1)
                act.wait_ge(wsum_copied, t + 1)
                act.dma_start(hid_d[bass.ds(t * P, P), :], sums[:, par, :]).then_inc(sums_out[par], 16)

            def products(par, extent):
                def slot(s, n, column, free, arrived):
                    act.wait_ge(weight_ready[par], n + 1)
                    act.wait_ge(prod_free[par], free)
                    for h in range(DVE_HEADS, HEADS):
                        m = act.activation(prod[:, par, s, h * DH:(h + 1) * DH], near[:, par, s, h * DH:(h + 1) * DH],
                                           ACT.Copy, scale=weight[:, par, s, h:h + 1])
                    m.then_inc(act_done[par], 1)

                slots_of(act, extent, slot)

            even, odd = extents(act, 0)
            products(0, even)
            products(1, odd)
            columns(0, 0, True)
            even, odd = extents(act, 1)
            products(0, even)
            columns(1, 1, True)
            rows(0, 0, 0, True)
            products(1, odd)
            columns(2, 0, False)
            rows(1, 0, 1, True)
            with act.Fori(2, NT // 2) as tt:
                even, odd = extents(act, tt)
                products(0, even)
                columns(2 * tt - 1, 1, False)
                rows(2 * tt - 2, tt - 1, 0, False)
                products(1, odd)
                columns(2 * tt, 0, False)
                rows(2 * tt - 1, tt - 1, 1, False)
            columns(NT - 1, 1, False)
            rows(NT - 2, NT // 2 - 1, 0, False)
            rows(NT - 1, NT // 2 - 1, 1, False)
            for par in range(2):
                act.wait_ge(sums_out[par], 16 * (NT // 2))


def hard_rows(nc, adj, seq_d, rec_d, hid_d, identf, ones, powers, ctrl, N, D, NT, ROW):
    DH = D // HEADS
    QUAD = 4
    PAIRS = HEADS // 2
    PIECES = P // UNIT
    PT = NT // PIECES
    QUAD_P = 32
    LOADS = HEADS // QUAD
    with ExitStack() as ctx:
        def sb(name, shape, dt):
            return ctx.enter_context(nc.sbuf_tensor(name, shape, dt))

        def ps(name, shape, dt):
            return ctx.enter_context(nc.psum_tensor(name, shape, dt))

        def sem(name):
            return ctx.enter_context(nc.semaphore(name))

        urec = sb("urec", [UNIT, R_ALL], F32)
        piece_i = sb("piece_i", [P, 2], I32)
        piece = sb("piece", [P, 1], F32)
        of_row = sb("of_row", [P, 2], F32)
        piece_at = sb("piece_at", [P, 1], U32)
        uadj = sb("uadj", [P, PT * P], F32)
        uadjT = sb("uadjT", [P, NT, UNIT], F32)
        diag = sb("diag", [UNIT, 2, HEADS, UNIT], F32)
        factor = sb("factor", [P, 2, HEADS, UNIT], F32)
        values = sb("values", [P, 2, NT, QUAD * DH], F32)
        pos = sb("pos_w", [P, NT, 2, UNIT], F32)
        neg = sb("neg_w", [P, NT, 2, UNIT], F32)
        weight = sb("unit_weight", [P, 2, NT, 2, QUAD_P], F32)
        part_sum = sb("part_sum", [P, HEADS, UNIT], F32)
        uhid = sb("uhid", [UNIT, ROW], F32)
        adjT_ps = ps("uadjT_ps", [P, PT, UNIT, PIECES], F32)
        factor_ps = ps("factor_ps", [P, 2, HEADS * UNIT], F32)
        pair_ps = ps("pair_ps", [2 * QUAD_P, 2, 512], F32)
        total_ps = ps("total_ps", [UNIT, HEADS], F32)

        urec_in = sem("urec_in")
        of_row_in = sem("of_row_in")
        piece_made = sem("piece_made")
        piece_ready = sem("piece_ready")
        weight_clear = sem("weight_clear")
        uadj_in = sem("uadj_in")
        diag_ready = sem("diag_ready")
        lone_fixed = sem("lone_fixed")
        spread = sem("spread")
        turned = sem("turned")
        copied = sem("copied")
        values_in = [sem("values_in0"), sem("values_in1")]
        part_ready = sem("part_ready")
        weight_ready = sem("uweight_ready")
        sum_ready = sem("sum_ready")
        pair_done = sem("pair_done")
        pair_copied = sem("pair_copied")
        totalled = sem("totalled")
        unit_copied = sem("unit_copied")
        unit_out = sem("unit_out")
        carried = sem("carried_u")

        block = ctx.enter_context(nc.Block())
        seq_v = seq_d.rearrange("(t p) c -> p t c", p=P)
        adj_pieces = adj.rearrange("n (q c) -> (n q) c", q=PIECES)

        def number(eng):
            return eng.value_load(ctrl[0:1, 4 * NT:4 * NT + 1], min_val=1, max_val=N // UNIT)

        def first_row(d):
            return d * -UNIT + (N - UNIT)

        @block.sync
        def _(sp):
            count = number(sp)
            with sp.Fori(0, count) as d:
                sp.dma_start(of_row[:, :], rec_d[bass.ds(first_row(d), UNIT), R_SELF:R_SELF + 2].rearrange("i (o c) -> i o c", o=1
                             ).broadcast_to([UNIT, PIECES, 2])).then_inc(of_row_in, 16)
                sp.dma_start(urec[:, :], rec_d[bass.ds(first_row(d), UNIT), :]).then_inc(urec_in, 16)
                sp.wait_ge(uadj_in, (d + 1) * 16)
                sp.sem_inc(carried, 1)
                for q in range(LOADS):
                    if q >= 2:
                        sp.wait_ge(pair_done, d * PAIRS + (2 * (q - 1) + 2))
                        sp.sem_inc(carried, 1)
                    sp.dma_start(values[:, q % 2, :, :], seq_v[:, :, q * QUAD * DH:(q + 1) * QUAD * DH]
                                 ).then_inc(values_in[q % 2], 16)
                sp.wait_ge(unit_copied, d + 1)
                sp.sem_inc(carried, 1)
                sp.dma_start(hid_d[bass.ds(first_row(d), UNIT), :], uhid[:, :]).then_inc(unit_out, 16)
                sp.wait_ge(unit_out, (d + 1) * 16)
                sp.sem_inc(carried, 1)

        @block.gpsimd
        def _(pool):
            count = number(pool)
            pool.iota(piece_i[:, :], pattern=[[0, 2]], base=0, channel_multiplier=1).then_inc(piece_made, 1)
            pool.sem_inc(pair_done, 2)
            pool.sem_inc(pair_copied, 2)
            with pool.Fori(0, count) as d:
                pool.wait_ge(piece_ready, d + 1)
                pool.sem_inc(carried, 1)
                pool.indirect_dma_start(uadj[:, :], None, adj_pieces,
                                        bass.IndirectOffsetOnAxis(ap=piece_at[:, 0:1], axis=0),
                                        bounds_check=N * PIECES - 1).then_inc(uadj_in, 16)

        @block.vector
        def _(dve):
            count = number(dve)
            dve.memset(weight[:, :, :, :, :], 0.0).then_inc(weight_clear, 1)
            dve.wait_ge(piece_made, 1)
            dve.tensor_scalar(piece_i[:, 1:2], piece_i[:, 0:1], PIECES - 1, None, ALU.bitwise_and)
            dve.drain()
            dve.tensor_copy(piece[:, :], piece_i[:, 1:2])
            dve.drain()
            with dve.Fori(0, count) as d:
                dve.wait_ge(of_row_in, (d + 1) * 16)
                dve.scalar_tensor_tensor(piece_at[:, :], of_row[:, 0:1].bitcast(U32), float(PIECES), piece[:, :],
                                         ALU.mult, ALU.add).then_inc(piece_ready, 1)
                dve.wait_ge(urec_in, (d + 1) * 16)
                for s, col in enumerate((R_A, R_C)):
                    dve.tensor_tensor(diag[:, s, :, :],
                                      urec[:, col:col + HEADS].rearrange("p (h o) -> p h o", o=1).broadcast_to([UNIT, HEADS, UNIT]),
                                      identf[0:UNIT, 0:UNIT].rearrange("p (o i) -> p o i", o=1).broadcast_to([UNIT, HEADS, UNIT]),
                                      ALU.mult).then_inc(diag_ready, 1)
                dve.wait_ge(uadj_in, (d + 1) * 16)
                dve.tensor_scalar(uadj[:, :], uadj[:, :], of_row[:, 1:2], None, ALU.max).then_inc(lone_fixed, 1)
                dve.wait_ge(spread, d + 1)
                dve.tensor_copy(factor[:, :, :, :].rearrange("p s h i -> p s (h i)"), factor_ps[:, :, :]).then_inc(copied, 1)
                dve.wait_ge(turned, d + 1)
                dve.tensor_copy(uadjT[:, :, :].rearrange("p (q c) i -> p q c i", q=PIECES),
                                adjT_ps[:, :, :, :].rearrange("p c i q -> p q c i")).then_inc(copied, 1)
                dve.wait_ge(copied, d * 2 + 2)
                dve.sem_inc(carried, 1)

                with dve.Fori(0, PAIRS // 2) as pp:
                    for b in range(2):
                        pair = 2 * pp + b
                        n = d * (3 * PAIRS) + pair * 3
                        for part, s in ((pos, 0), (neg, 1)):
                            dve.tensor_tensor(part[:, :, :, :],
                                              factor[:, s:s + 1, bass.ds(2 * pair, 2), :].broadcast_to([P, NT, 2, UNIT]),
                                              powers[:, :, s, bass.ds(2 * pair, 2)].rearrange("p t (h o) -> p t h o", o=1
                                                                                              ).broadcast_to([P, NT, 2, UNIT]),
                                              ALU.mult).then_inc(part_ready, 1)
                        dve.wait_ge(part_ready, n + 2)
                        dve.tensor_tensor(pos[:, :, :, :], pos[:, :, :, :], neg[:, :, :, :], ALU.max).then_inc(part_ready, 1)
                        dve.wait_ge(pair_done, d * PAIRS + (pair + 1))
                        dve.wait_ge(part_ready, n + 3)
                        dve.tensor_tensor(weight[:, b, :, :, 0:UNIT], pos[:, :, :, :],
                                          uadjT[:, :, :].rearrange("p t (o i) -> p t o i", o=1).broadcast_to([P, NT, 2, UNIT]),
                                          ALU.mult).then_inc(weight_ready, 1)
                        dve.wait_ge(weight_ready, d * PAIRS + (pair + 1))
                        dve.tensor_reduce(part_sum[:, bass.ds(2 * pair, 2), :],
                                          weight[:, b, :, :, 0:UNIT].rearrange("p t h i -> p h i t"), AX.X, ALU.add
                                          ).then_inc(sum_ready, 1)

        @block.tensor
        def _(pe):
            count = number(pe)
            pe.wait_ge(weight_clear, 1)
            with pe.Fori(0, count) as d:
                pe.wait_ge(diag_ready, d * 2 + 2)
                for s in range(2):
                    mm = pe.matmul(factor_ps[:, s, :], ones[0:UNIT, :], diag[:, s, :, :].rearrange("p h i -> p (h i)"),
                                   start=True, stop=True)
                mm.then_inc(spread, 1)
                pe.wait_ge(lone_fixed, d + 1)
                pe.sem_inc(carried, 1)
                for c in range(PT):
                    mm = pe.transpose(adjT_ps[:, c, :, :].rearrange("p i q -> p (i q)"), uadj[:, c * P:(c + 1) * P],
                                      identf[:, :])
                mm.then_inc(turned, 1)

                with pe.Fori(0, LOADS // 2) as qq:
                    for v in range(2):
                        pe.wait_ge(values_in[v], (d * (LOADS // 2) + (qq + 1)) * 16)
                        for b in range(2):
                            pair = qq * 4 + (2 * v + b)
                            pe.wait_ge(weight_ready, d * PAIRS + (pair + 1))
                            pe.wait_ge(pair_copied, d * PAIRS + (pair + 1))
                            for j in range(NT):
                                mm = pe.matmul(pair_ps[:, b, 0:2 * DH], weight[:, b, j, :, :].rearrange("p h i -> p (h i)"),
                                               values[:, v, j, b * 2 * DH:(b + 1) * 2 * DH],
                                               start=(j == 0), stop=(j == NT - 1))
                            mm.then_inc(pair_done, 1)
                pe.wait_ge(sum_ready, (d + 1) * PAIRS)
                for h in range(HEADS):
                    mm = pe.matmul(total_ps[:, h:h + 1], part_sum[:, h, :], ones[:, 0:1], start=True, stop=True)
                mm.then_inc(totalled, 1)

        @block.scalar
        def _(act):
            count = number(act)
            with act.Fori(0, count) as d:
                with act.Fori(0, PAIRS // 2) as pp:
                    for b in range(2):
                        pair = 2 * pp + b
                        act.wait_ge(pair_done, d * PAIRS + (pair + 3))
                        for h in range(2):
                            cp = act.copy(uhid[:, bass.ds(pair * (2 * DH) + h * DH, DH)],
                                          pair_ps[h * QUAD_P:h * QUAD_P + UNIT, b, h * DH:(h + 1) * DH])
                        cp.then_inc(pair_copied, 1)
                act.wait_ge(totalled, d + 1)
                act.copy(uhid[:, D:ROW], total_ps[:, :]).then_inc(unit_copied, 1)


def output_layer(nc, x, w_hi, w_lo, b_out, rec_d, hid_d, out, identf, N, D, NT, KT, ROW):
    DH = D // HEADS
    CH = D // 512
    with ExitStack() as ctx:
        def sb(name, shape, dt):
            return ctx.enter_context(nc.sbuf_tensor(name, shape, dt))

        def sem(name):
            return ctx.enter_context(nc.semaphore(name))

        bias = sb("bias", [P, D], F32)
        hid = sb("hid", [P, 2, ROW], F32)
        recip = sb("recip", [P, 2, HEADS], F32)
        normed = sb("normed", [P, 2, D], F32)
        own = sb("own", [P, NT, R_ALL - R_SELF], U32)
        own_t = sb("own_t", [P, 2], U32)
        own_s = sb("own_s", [P, 2], U32)
        xin = sb("x_res", [P, 2, D], F32)
        hT_hi = sb("hT_hi", [P, 2, KT, P], F16)
        hT_lo = sb("hT_lo", [P, 2, KT, P], F16)
        z = sb("z", [P, 2, D], F32)
        neg = sb("neg", [P, 2, D], F32)
        e = sb("e", [P, 2, D], F32)
        y = sb("y", [P, 2, D], F32)
        fin = sb("fin", [P, 2, D], F32)
        pos = sb("pos", [P, 2, D], F32)
        stats = sb("stats", [P, 2, CH, 6], F32)
        mv = sb("mv", [P, 2, 2], F32)
        var = sb("var", [P, 2], F32)
        rstd = sb("rstd", [P, 2], F32)
        hT_ps = ctx.enter_context(nc.psum_tensor("hT_ps", [P, KT, P], F32))
        z_ps = ctx.enter_context(nc.psum_tensor("z_ps", [P, 2, CH, 512], F32))

        half = sb("half", [P, 2], F32)
        b_in = sem("b_in")
        const_made = sem("const_made")
        hid_in = [sem("hid_in0"), sem("hid_in1")]
        x_in = [sem("x_res0"), sem("x_res1")]
        own_in = sem("own_in")
        carried = sem("carried_o")
        own_ready = sem("own_ready")
        own_s_ready = sem("own_s_ready")
        recip_ready = sem("recip_ready")
        normalised = sem("normalised")
        h_turned = sem("h_turned")
        hT_high = sem("hT_high")
        hT_copied = sem("hT_copied")
        z_done = sem("z_done")
        z_ready = sem("z_ready")
        neg_ready = sem("neg_ready")
        exp_ready = sem("exp_ready")
        pos_ready = sem("pos_ready")
        y_ready = sem("y_ready")
        stats_ready = sem("stats_ready")
        mv_ready = sem("mv_ready")
        var_ready = sem("var_ready")
        rstd_ready = sem("rstd_ready")
        fin_ready = sem("fin_ready")
        out_stored = [sem("out0"), sem("out1")]

        block = ctx.enter_context(nc.Block())

        @block.sync
        def _(sp):
            sp.dma_start(own[:, :, :], rec_d[:, R_SELF:R_ALL].bitcast(U32).rearrange("(t p) c -> p t c", p=P)).then_inc(own_in, 16)

            def load(t, par, first):
                if not first:
                    sp.wait_ge(normalised, t - 1)
                sp.dma_start(hid[:, par, :], hid_d[bass.ds(t * P, P), :]).then_inc(hid_in[par], 16)

            load(0, 0, True)
            load(1, 1, True)
            sp.dma_start(bias[:, :], b_out.partition_broadcast(P)).then_inc(b_in, 16)
            with sp.Fori(1, NT // 2) as tt:
                for par in range(2):
                    load(2 * tt + par, par, False)

        @block.tensor
        def _(pe):
            def turn(t, tt, par, very_first):
                pe.wait_ge(normalised, t + 1)
                if not very_first:
                    pe.wait_ge(hT_copied, t)
                for k in range(KT):
                    mm = pe.transpose(hT_ps[:, k, :], normed[:, par, k * P:(k + 1) * P], identf[:, :])
                mm.then_inc(h_turned, 1)

            def project(t, par, first):
                pe.wait_ge(hT_copied, t + 1)
                if not first:
                    pe.wait_ge(z_ready, t - 1)
                for k in range(KT):
                    for c in range(CH):
                        for part in (w_hi, w_lo):
                            pe.matmul(z_ps[:, par, c, :], hT_hi[:, par, k, :], part[:, k, c * 512:(c + 1) * 512],
                                      start=(k == 0 and part is w_hi), stop=False)
                    for c in range(CH):
                        mm = pe.matmul(z_ps[:, par, c, :], hT_lo[:, par, k, :], w_hi[:, k, c * 512:(c + 1) * 512],
                                       start=False, stop=(k == KT - 1))
                mm.then_inc(z_done, 1)

            turn(0, 0, 0, True)
            turn(1, 0, 1, False)
            project(0, 0, True)
            turn(2, 1, 0, False)
            project(1, 1, True)
            turn(3, 1, 1, False)
            project(2, 0, False)
            with pe.Fori(2, NT // 2) as tt:
                turn(2 * tt, tt, 0, False)
                project(2 * tt - 1, 1, False)
                turn(2 * tt + 1, tt, 1, False)
                project(2 * tt, 0, False)
            project(NT - 1, 1, False)

        @block.vector
        def _(dve):
            def normalise(t, tt, par, first):
                dve.wait_ge(hid_in[par], 16 * (tt + 1))
                dve.reciprocal(recip[:, par, :], hid[:, par, D:ROW]).then_inc(recip_ready, 1)
                if not first:
                    dve.wait_ge(h_turned, t - 1)
                dve.wait_ge(recip_ready, t + 1)
                dve.tensor_tensor(normed[:, par, :].rearrange("p (h d) -> p h d", h=HEADS),
                                  hid[:, par, 0:D].rearrange("p (h d) -> p h d", h=HEADS),
                                  recip[:, par, :].rearrange("p (h o) -> p h o", o=1).broadcast_to([P, HEADS, DH]),
                                  ALU.mult).then_inc(normalised, 1)

            def copy_hT(t, par, first):
                if not first:
                    dve.wait_ge(z_done, t - 1)
                dve.wait_ge(hT_high, t + 1)
                dve.scalar_tensor_tensor(hT_lo[:, par, :, :], hT_ps[:, :, :], H_LIFT, hT_hi[:, par, :, :],
                                         ALU.mult, ALU.subtract).then_inc(hT_copied, 1)

            def finish(t, tt, par, first):
                dve.wait_ge(rstd_ready, t + 1)
                if not first:
                    dve.wait_ge(out_stored[par], 16 * tt)
                dve.tensor_scalar(fin[:, par, :], y[:, par, :], mv[:, par, 0:1], rstd[:, par:par + 1],
                                  ALU.subtract, ALU.mult).then_inc(fin_ready, 1)

            def tile(t, tt, par, first, very_first, left):
                if left >= 1:
                    copy_hT(t + 1, 1 - par, very_first)
                if left >= 2:
                    normalise(t + 2, tt + 1, par, False)
                dve.wait_ge(z_done, t + 1)
                dve.scalar_tensor_tensor(z[:, par, :].rearrange("p (c f) -> p c f", c=CH), z_ps[:, par, :, :],
                                         1.0 / (W_LIFT * H_LIFT), bias[:, :].rearrange("p (c f) -> p c f", c=CH),
                                         ALU.mult, ALU.add).then_inc(z_ready, 1)
                dve.wait_ge(z_ready, t + 1)
                dve.tensor_scalar(neg[:, par, :], z[:, par, :], 0.0, None, ALU.min).then_inc(neg_ready, 1)
                dve.wait_ge(x_in[par], 16 * (tt + 1))
                dve.scalar_tensor_tensor(pos[:, par, :], z[:, par, :], 0.0, xin[:, par, :],
                                         ALU.max, ALU.add).then_inc(pos_ready, 1)
                if not very_first:
                    finish(t - 1, tt if par else tt - 1, 1 - par, first)
                dve.wait_ge(exp_ready, t + 1)
                dve.wait_ge(pos_ready, t + 1)
                dve.scalar_tensor_tensor(y[:, par, :], e[:, par, :], -1.0, pos[:, par, :],
                                         ALU.add, ALU.add).then_inc(y_ready, 1)
                dve.wait_ge(y_ready, t + 1)
                for c in range(CH):
                    dve.bn_stats(stats[:, par, c, :], y[:, par, c * 512:(c + 1) * 512]).then_inc(stats_ready, 1)
                dve.drain()
                dve.bn_aggr(mv[:, par, :], stats[:, par, :, :]).then_inc(mv_ready, 1)
                dve.wait_ge(mv_ready, t + 1)
                dve.tensor_scalar(var[:, par:par + 1], mv[:, par, 1:2], EPS, None, ALU.add).then_inc(var_ready, 1)

            normalise(0, 0, 0, True)
            normalise(1, 0, 1, True)
            copy_hT(0, 0, True)
            dve.wait_ge(b_in, 16)
            tile(0, 0, 0, True, True, 2)
            tile(1, 0, 1, True, False, 2)
            tile(2, 1, 0, True, False, 2)
            tile(3, 1, 1, False, False, 2)
            with dve.Fori(2, NT // 2 - 1) as tt:
                tile(2 * tt, tt, 0, False, False, 2)
                tile(2 * tt + 1, tt, 1, False, False, 2)
            tile(NT - 2, NT // 2 - 1, 0, False, False, 1)
            tile(NT - 1, NT // 2 - 1, 1, False, False, 0)
            finish(NT - 1, NT // 2 - 1, 1, False)

        @block.scalar
        def _(act):
            def tile(t, par, first):
                act.wait_ge(neg_ready, t + 1)
                if not first:
                    act.wait_ge(y_ready, t - 1)
                act.activation(e[:, par, :], neg[:, par, :], ACT.Exp).then_inc(exp_ready, 1)

            def high(t, par, first):
                act.wait_ge(h_turned, t + 1)
                if not first:
                    act.wait_ge(z_done, t - 1)
                act.activation(hT_hi[:, par, :, :], hT_ps[:, :, :], ACT.Copy, scale=H_LIFT).then_inc(hT_high, 1)

            high(0, 0, True)
            high(1, 1, True)
            tile(0, 0, True)
            high(2, 0, False)
            tile(1, 1, True)
            high(3, 1, False)
            with act.Fori(1, NT // 2 - 1) as tt:
                tile(2 * tt, 0, False)
                high(2 * tt + 2, 0, False)
                tile(2 * tt + 1, 1, False)
                high(2 * tt + 3, 1, False)
            tile(NT - 2, 0, False)
            tile(NT - 1, 1, False)

        @block.gpsimd
        def _(pool):
            pool.memset(half[:, 0:1], -0.5).then_inc(const_made, 1)
            pool.wait_ge(const_made, 1)

            def gather(t, par, first):
                if not first:
                    pool.wait_ge(pos_ready, t - 1)
                pool.tensor_copy(own_t[:, par:par + 1], own[:, bass.ds(t, 1), 0]).then_inc(own_ready, 1)
                pool.wait_ge(own_ready, t + 1)
                pool.sem_inc(carried, 1)
                pool.indirect_dma_start(xin[:, par, :], None, x,
                                        bass.IndirectOffsetOnAxis(ap=own_t[:, par:par + 1], axis=0),
                                        bounds_check=N - 1).then_inc(x_in[par], 16)

            def root(t, par, first):
                pool.wait_ge(var_ready, t + 1)
                if not first:
                    pool.wait_ge(fin_ready, t - 1)
                pool.tensor_tensor(rstd[:, par:par + 1], var[:, par:par + 1], half[:, 0:1], ALU.pow).then_inc(rstd_ready, 1)

            def scatter(t, tt, par, first):
                if not first:
                    pool.wait_ge(out_stored[par], 16 * tt)
                pool.tensor_copy(own_s[:, par:par + 1], own[:, bass.ds(t, 1), 0]).then_inc(own_s_ready, 1)
                pool.wait_ge(fin_ready, t + 1)
                pool.wait_ge(own_s_ready, t + 1)
                pool.sem_inc(carried, 1)
                pool.indirect_dma_start(out, bass.IndirectOffsetOnAxis(ap=own_s[:, par:par + 1], axis=0),
                                        fin[:, par, :], None, bounds_check=N - 1).then_inc(out_stored[par], 16)

            pool.wait_ge(own_in, 16)
            gather(0, 0, True)
            gather(1, 1, True)
            gather(2, 0, False)
            root(0, 0, True)
            gather(3, 1, False)
            root(1, 1, True)
            scatter(0, 0, 0, True)
            gather(4, 0, False)
            root(2, 0, False)
            scatter(1, 0, 1, True)
            gather(5, 1, False)
            root(3, 1, False)
            scatter(2, 1, 0, False)
            with pool.Fori(2, NT // 2 - 1) as tt:
                gather(2 * tt + 2, 0, False)
                root(2 * tt, 0, False)
                scatter(2 * tt - 1, tt - 1, 1, False)
                gather(2 * tt + 3, 1, False)
                root(2 * tt + 1, 1, False)
                scatter(2 * tt, tt, 0, False)
            root(NT - 2, 0, False)
            scatter(NT - 3, NT // 2 - 2, 1, False)
            root(NT - 1, 1, False)
            scatter(NT - 2, NT // 2 - 1, 0, False)
            scatter(NT - 1, NT // 2 - 1, 1, False)
            pool.wait_ge(out_stored[0], 16 * (NT // 2))
            pool.wait_ge(out_stored[1], 16 * (NT // 2))


_INS = ["x", "adj", "L0_gnn_W_seq", "L0_gnn_a1", "L0_gnn_a2", "L0_gnn_W_out", "L0_gnn_b_out"]


def kernel(**inputs):
    import numpy as np
    import concourse.bacc as bacc
    from concourse.bass_utils import run_bass_kernel_spmd

    nc = bacc.Bacc("TRN2", target_bir_lowering=False, num_devices=1)
    arrays, args = {}, []
    for name in _INS:
        a = np.ascontiguousarray(inputs[name])
        arrays[f"in_{name}_dram"] = a
        args.append(nc.dram_tensor(f"in_{name}_dram", a.shape, mybir.dt.from_np(a.dtype), kind="ExternalInput").ap())
    shape = inputs["x"].shape
    args.append(nc.dram_tensor("out_0_dram", shape, F32, kind="ExternalOutput").ap())
    gat_layer(nc, *args)
    r = run_bass_kernel_spmd(nc, [arrays], core_ids=[0])
    return r.results[0]["out_0_dram"]
```
